# Optimizing a Trainium2 kernel written in Bass

```python
import numpy as np
import jax
import jax.numpy as jnp

def _softmax(x, axis=-1):
    return jax.nn.softmax(x, axis=axis)

def _gelu(x):
    return jax.nn.gelu(x, approximate=True)

def _silu(x):
    return jax.nn.silu(x)

def _sigmoid(x):
    return jax.nn.sigmoid(x)

def _layernorm(x, axis=-1, eps=1e-05):
    m = jnp.mean(x, axis=axis, keepdims=True)
    v = jnp.var(x, axis=axis, keepdims=True)
    return (x - m) / jnp.sqrt(v + eps)

def _scatter_add(tgt, idx, src, axis=0):
    return tgt.at[idx].add(src)

def _segment_sum(src, seg, n):
    return jax.ops.segment_sum(src, seg, n)
kernel_name = 'mk_gnn_ffn_d2_gnn_r8_ff747d'

def setup_inputs(seed: int=0):
    np.random.seed(seed)
    _w = jnp.asarray

    def _rec_inputs():
        import jax
        import jax.numpy as jnp
        _gk = jax.random.key(seed)
        x = -0.0003713 + 1 * jax.random.normal(jax.random.fold_in(_gk, 1), (6250, 256), jnp.float32)
        src = jax.random.randint(jax.random.fold_in(_gk, 2), (200000,), 0, 6250, jnp.int32)
        dst = jnp.minimum((6250 * jax.random.uniform(jax.random.fold_in(_gk, 3), (200000,)) ** 2.0).astype(jnp.int32), 49999)
        _o = jnp.argsort(dst, stable=True)
        src = src[_o]
        dst = dst[_o]
        edge_attr_128 = 9.41057e-06 + 1 * jax.random.normal(jax.random.fold_in(_gk, 12), (200000, 128), jnp.float32)
        node_vec1 = jax.random.uniform(jax.random.fold_in(_gk, 14), (6250, 1), jnp.float32, 0.0, 0.999973)
        node_vec1_n2 = jax.random.uniform(jax.random.fold_in(_gk, 15), (6250, 1), jnp.float32, 0.0, 0.999973)
        return (x, src, dst, edge_attr_128, node_vec1, node_vec1_n2)
    x, src, dst, edge_attr_128, node_vec1, node_vec1_n2 = _rec_inputs()

    def _L0_gnn_setup():
        import jax, jax.numpy as jnp
        import numpy as np
        NUM_NODES = 6250
        NUM_EDGES = 200000
        NODE_DIM = 256
        EDGE_DIM = 128
        MAX_IN_DEGREE = 512
        MAX_OUT_DEGREE = 512
        key = jax.random.key(seed)
        ks = jax.random.split(key, 12)
        x = jax.random.normal(ks[0], (NUM_NODES, NODE_DIM), dtype=jnp.float32)
        edge_index = jax.random.randint(ks[1], (2, NUM_EDGES), 0, NUM_NODES, dtype=jnp.int64 if jax.config.read('jax_enable_x64') else jnp.int32)
        edge_attr = jax.random.normal(ks[2], (NUM_EDGES, EDGE_DIM), dtype=jnp.float32)
        voronoi_values = jax.random.uniform(ks[3], (NUM_NODES, 1), dtype=jnp.float32)
        centralities = jax.random.uniform(ks[4], (NUM_NODES, 1), dtype=jnp.float32)
        z_in = jax.random.normal(ks[5], (MAX_IN_DEGREE, NODE_DIM), dtype=jnp.float32)
        z_out = jax.random.normal(ks[6], (MAX_OUT_DEGREE, NODE_DIM), dtype=jnp.float32)
        W_cent = jax.random.normal(ks[7], (1, NODE_DIM), dtype=jnp.float32) * 0.5
        b_cent = jnp.zeros((NODE_DIM,), dtype=jnp.float32)
        W_vor = jax.random.normal(ks[8], (1, NODE_DIM), dtype=jnp.float32) * 0.5
        b_vor = jnp.zeros((NODE_DIM,), dtype=jnp.float32)
        W_sum = jax.random.normal(ks[9], (EDGE_DIM, NODE_DIM), dtype=jnp.float32) * (1.0 / np.sqrt(EDGE_DIM))
        b_sum = jnp.zeros((NODE_DIM,), dtype=jnp.float32)
        return {'x': x, 'edge_index': edge_index, 'edge_attr': edge_attr, 'voronoi_values': voronoi_values, 'centralities': centralities, 'z_in': z_in, 'z_out': z_out, 'W_cent': W_cent, 'b_cent': b_cent, 'W_vor': W_vor, 'b_vor': b_vor, 'W_sum': W_sum, 'b_sum': b_sum}
    _L0_gnn_all = _L0_gnn_setup()
    _L0_gnn_in = {k: v for k, v in _L0_gnn_all.items() if k in ('z_in', 'z_out', 'W_cent', 'b_cent', 'W_vor', 'b_vor', 'W_sum', 'b_sum')}
    del _L0_gnn_all

    def _L0_ffn_setup():
        import jax, jax.numpy as jnp
        import numpy as np
        NUM_EXPERTS = 8
        TOP_K = 2
        B, S, D = (8, 1024, 256)

        def _moe(tokens, router_w, w1, b1, w2, b2):
            N = tokens.shape[0]
            E = router_w.shape[0]
            logits = tokens.astype(jnp.float32) @ router_w.astype(jnp.float32).T
            probs = jax.nn.softmax(logits, axis=-1)
            rw, re = jax.lax.top_k(probs, TOP_K)
            if TOP_K > 1:
                rw = rw / jnp.maximum(rw.sum(-1, keepdims=True), 1e-12)
            rw = rw.astype(tokens.dtype)
            combine = jnp.zeros((N, E), tokens.dtype).at[jnp.arange(N)[:, None], re].set(rw)
            out = tokens
            for e in range(E):
                h = jax.nn.gelu(tokens @ w1[e] + b1[e], approximate=False)
                y = h @ w2[e] + b2[e]
                out = out + combine[:, e:e + 1] * y
            return out
        key = jax.random.key(seed)
        ks = jax.random.split(key, 4)
        scale = 1.0 / np.sqrt(D).astype(np.float32)
        return {'input_embeddings': jax.random.normal(ks[0], (B, S, D), jnp.float32), 'router_w': jax.random.normal(ks[1], (NUM_EXPERTS, D), jnp.float32) * scale, 'w1': jax.random.normal(ks[2], (NUM_EXPERTS, D, D), jnp.float32) * scale, 'b1': jnp.zeros((NUM_EXPERTS, D), jnp.float32), 'w2': jax.random.normal(ks[3], (NUM_EXPERTS, D, D), jnp.float32) * scale, 'b2': jnp.zeros((NUM_EXPERTS, D), jnp.float32)}
    _L0_ffn_all = _L0_ffn_setup()
    _L0_ffn_in = {k: v for k, v in _L0_ffn_all.items() if k in ('router_w', 'w1', 'b1', 'w2', 'b2')}
    del _L0_ffn_all

    def _L1_gnn_setup():
        import jax, jax.numpy as jnp
        import numpy as np
        N = 6250
        E = 100000
        HIDDEN = 256
        HEADS = 8
        HEAD_DIM = HIDDEN // HEADS

        def _linear_params(key, fan_in, fan_out):
            k1, k2 = jax.random.split(key)
            s = 1.0 / np.sqrt(fan_in)
            W = jax.random.uniform(k1, (fan_in, fan_out), jnp.float32, -s, s)
            b = jax.random.uniform(k2, (fan_out,), jnp.float32, -s, s)
            return (W, b)
        key = jax.random.key(seed)
        ks = jax.random.split(key, 7)
        h = jax.random.normal(ks[0], (N, HIDDEN), jnp.float32)
        row = jnp.sort(jax.random.randint(ks[1], (E,), 0, N))
        col = jax.random.randint(ks[2], (E,), 0, N)
        Wq, bq = _linear_params(ks[3], HIDDEN, HIDDEN)
        Wk, bk = _linear_params(ks[4], HIDDEN, HIDDEN)
        Wv, bv = _linear_params(ks[5], HIDDEN, HIDDEN)
        Wo, bo = _linear_params(ks[6], HIDDEN, HIDDEN)
        return dict(h=h, row=row, col=col, Wq=Wq, bq=bq, Wk=Wk, bk=bk, Wv=Wv, bv=bv, Wo=Wo, bo=bo)
    _L1_gnn_all = _L1_gnn_setup()
    _L1_gnn_in = {k: v for k, v in _L1_gnn_all.items() if k in ('Wq', 'bq', 'Wk', 'bk', 'Wv', 'bv', 'Wo', 'bo')}
    del _L1_gnn_all

    def _L1_ffn_setup():
        import math
        import jax, jax.numpy as jnp
        import numpy as np
        CAPACITY_FACTOR = 1.25
        TOP_K = 2
        LN_EPS = 1e-05

        def _layer_norm(x, gamma, beta):
            mu = jnp.mean(x, axis=-1, keepdims=True)
            var = jnp.var(x, axis=-1, keepdims=True)
            return (x - mu) * jax.lax.rsqrt(var + LN_EPS) * gamma + beta
        key = jax.random.key(seed)
        ks = jax.random.split(key, 4)
        B, S, D, F, E = (8, 512, 256, 512, 8)
        x = jax.random.normal(ks[0], (B, S, D), dtype=jnp.float32)
        Wr = jax.random.normal(ks[1], (D, E), dtype=jnp.float32) / np.sqrt(D)
        br = jnp.zeros((E,), jnp.float32)
        W1 = jax.random.normal(ks[2], (E, D, F), dtype=jnp.float32) / np.sqrt(D)
        b1 = jnp.zeros((E, F), jnp.float32)
        W2 = jax.random.normal(ks[3], (E, F, D), dtype=jnp.float32) / np.sqrt(F)
        b2 = jnp.zeros((E, D), jnp.float32)
        gamma = jnp.ones((D,), jnp.float32)
        beta = jnp.zeros((D,), jnp.float32)
        return {'x': x, 'Wr': Wr, 'br': br, 'W1': W1, 'b1': b1, 'W2': W2, 'b2': b2, 'gamma': gamma, 'beta': beta}
    _L1_ffn_all = _L1_ffn_setup()
    _L1_ffn_in = {k: v for k, v in _L1_ffn_all.items() if k in ('Wr', 'br', 'W1', 'b1', 'W2', 'b2', 'gamma', 'beta')}
    del _L1_ffn_all
    return {'x': x, 'src': src, 'dst': dst, 'edge_attr_128': edge_attr_128, 'node_vec1': node_vec1, 'node_vec1_n2': node_vec1_n2, 'L0_gnn_z_in': _L0_gnn_in['z_in'], 'L0_gnn_z_out': _L0_gnn_in['z_out'], 'L0_gnn_W_cent': _L0_gnn_in['W_cent'], 'L0_gnn_b_cent': _L0_gnn_in['b_cent'], 'L0_gnn_W_vor': _L0_gnn_in['W_vor'], 'L0_gnn_b_vor': _L0_gnn_in['b_vor'], 'L0_gnn_W_sum': _L0_gnn_in['W_sum'], 'L0_gnn_b_sum': _L0_gnn_in['b_sum'], 'L0_ffn_router_w': _L0_ffn_in['router_w'], 'L0_ffn_w1': _L0_ffn_in['w1'], 'L0_ffn_b1': _L0_ffn_in['b1'], 'L0_ffn_w2': _L0_ffn_in['w2'], 'L0_ffn_b2': _L0_ffn_in['b2'], 'L1_gnn_Wq': _L1_gnn_in['Wq'], 'L1_gnn_bq': _L1_gnn_in['bq'], 'L1_gnn_Wk': _L1_gnn_in['Wk'], 'L1_gnn_bk': _L1_gnn_in['bk'], 'L1_gnn_Wv': _L1_gnn_in['Wv'], 'L1_gnn_bv': _L1_gnn_in['bv'], 'L1_gnn_Wo': _L1_gnn_in['Wo'], 'L1_gnn_bo': _L1_gnn_in['bo'], 'L1_ffn_Wr': _L1_ffn_in['Wr'], 'L1_ffn_br': _L1_ffn_in['br'], 'L1_ffn_W1': _L1_ffn_in['W1'], 'L1_ffn_b1': _L1_ffn_in['b1'], 'L1_ffn_W2': _L1_ffn_in['W2'], 'L1_ffn_b2': _L1_ffn_in['b2'], 'L1_ffn_gamma': _L1_ffn_in['gamma'], 'L1_ffn_beta': _L1_ffn_in['beta']}

def reference(x, src, dst, edge_attr_128, node_vec1, node_vec1_n2, L0_gnn_z_in, L0_gnn_z_out, L0_gnn_W_cent, L0_gnn_b_cent, L0_gnn_W_vor, L0_gnn_b_vor, L0_gnn_W_sum, L0_gnn_b_sum, L0_ffn_router_w, L0_ffn_w1, L0_ffn_b1, L0_ffn_w2, L0_ffn_b2, L1_gnn_Wq, L1_gnn_bq, L1_gnn_Wk, L1_gnn_bk, L1_gnn_Wv, L1_gnn_bv, L1_gnn_Wo, L1_gnn_bo, L1_ffn_Wr, L1_ffn_br, L1_ffn_W1, L1_ffn_b1, L1_ffn_W2, L1_ffn_b2, L1_ffn_gamma, L1_ffn_beta):
    import jax
    import jax.numpy as jnp

    def _L0_gnn_ref(x, edge_index, edge_attr, voronoi_values, centralities, z_in, z_out, W_cent, b_cent, W_vor, b_vor, W_sum, b_sum):
        import jax, jax.numpy as jnp
        import numpy as np
        NUM_NODES = 6250
        NUM_EDGES = 200000
        NODE_DIM = 256
        EDGE_DIM = 128
        MAX_IN_DEGREE = 512
        MAX_OUT_DEGREE = 512
        num_nodes = x.shape[0]
        src = edge_index[0]
        dst = edge_index[1]
        ones = jnp.ones_like(src, dtype=jnp.int32)
        in_deg = jnp.minimum(jax.ops.segment_sum(ones, dst, num_segments=num_nodes), MAX_IN_DEGREE - 1)
        out_deg = jnp.minimum(jax.ops.segment_sum(ones, src, num_segments=num_nodes), MAX_OUT_DEGREE - 1)
        edge_proj = edge_attr @ W_sum + b_sum
        sum3d = jax.ops.segment_sum(edge_proj, src, num_segments=num_nodes)
        cent_term = jax.nn.sigmoid(centralities @ W_cent + b_cent)
        vor_term = jax.nn.sigmoid(voronoi_values @ W_vor + b_vor)
        return x + z_in[in_deg] + z_out[out_deg] + cent_term + vor_term + sum3d

    def _L0_ffn_ref(input_embeddings, router_w, w1, b1, w2, b2):
        import jax, jax.numpy as jnp
        import numpy as np
        NUM_EXPERTS = 8
        TOP_K = 2
        B, S, D = (8, 1024, 256)

        def _moe(tokens, router_w, w1, b1, w2, b2):
            N = tokens.shape[0]
            E = router_w.shape[0]
            logits = tokens.astype(jnp.float32) @ router_w.astype(jnp.float32).T
            probs = jax.nn.softmax(logits, axis=-1)
            rw, re = jax.lax.top_k(probs, TOP_K)
            if TOP_K > 1:
                rw = rw / jnp.maximum(rw.sum(-1, keepdims=True), 1e-12)
            rw = rw.astype(tokens.dtype)
            combine = jnp.zeros((N, E), tokens.dtype).at[jnp.arange(N)[:, None], re].set(rw)
            out = tokens
            for e in range(E):
                h = jax.nn.gelu(tokens @ w1[e] + b1[e], approximate=False)
                y = h @ w2[e] + b2[e]
                out = out + combine[:, e:e + 1] * y
            return out
        b, s, d = input_embeddings.shape
        tokens = input_embeddings.reshape(b * s, d)
        return _moe(tokens, router_w, w1, b1, w2, b2).reshape(b, s, d)

    def _L1_gnn_ref(h, row, col, Wq, bq, Wk, bk, Wv, bv, Wo, bo):
        import jax, jax.numpy as jnp
        import numpy as np
        N = 6250
        E = 100000
        HIDDEN = 256
        HEADS = 8
        HEAD_DIM = HIDDEN // HEADS

        def _linear_params(key, fan_in, fan_out):
            k1, k2 = jax.random.split(key)
            s = 1.0 / np.sqrt(fan_in)
            W = jax.random.uniform(k1, (fan_in, fan_out), jnp.float32, -s, s)
            b = jax.random.uniform(k2, (fan_out,), jnp.float32, -s, s)
            return (W, b)
        n = h.shape[0]
        scaling = HEAD_DIM ** (-0.5)
        q = (h @ Wq + bq).reshape(n, HEADS, HEAD_DIM) * scaling
        k = (h @ Wk + bk).reshape(n, HEADS, HEAD_DIM)
        v = (h @ Wv + bv).reshape(n, HEADS, HEAD_DIM)
        s = jnp.einsum('ehd,ehd->eh', q[row], k[col])
        m = jax.ops.segment_max(s, row, num_segments=n)
        p = jnp.exp(s - m[row])
        denom = jax.ops.segment_sum(p, row, num_segments=n)
        attn = p / denom[row]
        out = jax.ops.segment_sum(attn[:, :, None] * v[col], row, num_segments=n)
        return out.reshape(n, HIDDEN) @ Wo + bo

    def _L1_ffn_ref(x, Wr, br, W1, b1, W2, b2, gamma, beta):
        import math
        import jax, jax.numpy as jnp
        import numpy as np
        CAPACITY_FACTOR = 1.25
        TOP_K = 2
        LN_EPS = 1e-05

        def _layer_norm(x, gamma, beta):
            mu = jnp.mean(x, axis=-1, keepdims=True)
            var = jnp.var(x, axis=-1, keepdims=True)
            return (x - mu) * jax.lax.rsqrt(var + LN_EPS) * gamma + beta
        B, S, D = x.shape
        E = Wr.shape[1]
        N = B * S
        K = TOP_K
        logits = jnp.mean(x, axis=1) @ Wr + br
        routing_weights = jax.nn.softmax(logits, axis=-1)
        capacity = float(math.ceil(N * CAPACITY_FACTOR / E))
        expected_loads = routing_weights.sum(axis=0) * (N / B)
        scale = jnp.where(expected_loads > capacity, capacity / expected_loads, 1.0)
        routing_weights = jax.nn.softmax(routing_weights * scale, axis=-1)
        rw_tok = jnp.broadcast_to(routing_weights[:, None, :], (B, S, E)).reshape(N, E)
        top_w, top_i = jax.lax.top_k(rw_tok, K)
        top_w = jax.nn.softmax(top_w, axis=-1)
        xf = x.reshape(N, D)
        h = jax.nn.gelu(jnp.einsum('nd,edf->enf', xf, W1) + b1[:, None, :], approximate=False)
        y = jnp.einsum('enf,efd->end', h, W2) + b2[:, None, :]
        w_dense = jnp.zeros((N, E), x.dtype).at[jnp.arange(N)[:, None], top_i].add(top_w)
        out = jnp.einsum('ne,end->nd', w_dense, y).reshape(B, S, D)
        out = _layer_norm(out + x, gamma, beta)
        return out
    edge_index = jnp.stack([src, dst])
    x = x + _L0_gnn_ref(_layernorm(x, axis=-1), edge_index, edge_attr_128, node_vec1, node_vec1_n2, L0_gnn_z_in, L0_gnn_z_out, L0_gnn_W_cent, L0_gnn_b_cent, L0_gnn_W_vor, L0_gnn_b_vor, L0_gnn_W_sum, L0_gnn_b_sum)
    x = x + _L0_ffn_ref(_layernorm(x, axis=-1)[None], L0_ffn_router_w, L0_ffn_w1, L0_ffn_b1, L0_ffn_w2, L0_ffn_b2)[0]
    x = x + _L1_gnn_ref(_layernorm(x, axis=-1), src, dst, L1_gnn_Wq, L1_gnn_bq, L1_gnn_Wk, L1_gnn_bk, L1_gnn_Wv, L1_gnn_bv, L1_gnn_Wo, L1_gnn_bo)
    x = x + _L1_ffn_ref(_layernorm(x, axis=-1)[None], L1_ffn_Wr, L1_ffn_br, L1_ffn_W1, L1_ffn_b1, L1_ffn_W2, L1_ffn_b2, L1_ffn_gamma, L1_ffn_beta)[0]
    return x

_drawn_inputs = setup_inputs


def setup_inputs(seed=0):
    import zlib

    import numpy as np

    out = dict(_drawn_inputs(seed))
    spreads = {'L0_gnn_b_cent': (0.0, 2.0),
     'L0_gnn_b_vor': (0.0, 2.0),
     'L0_gnn_b_sum': (0.0, 0.1),
     'L0_ffn_b1': (0.0, 0.8),
     'L0_ffn_b2': (0.0, 0.8),
     'L1_ffn_br': (0.0, 0.1),
     'L1_ffn_b1': (0.0, 0.8),
     'L1_ffn_b2': (0.0, 0.8),
     'L1_ffn_gamma': (1.0, 0.6),
     'L1_ffn_beta': (0.0, 0.752)}
    factors = {'node_vec1': 8.0,
     'node_vec1_n2': 8.0,
     'L0_gnn_W_cent': 5.411,
     'L0_gnn_W_vor': 5.584,
     'L1_gnn_Wq': 8.0,
     'L1_gnn_bq': 8.0,
     'L1_gnn_Wk': 8.0,
     'L1_gnn_bk': 64.0,
     'L1_gnn_Wv': 2.758,
     'L1_gnn_bv': 8.0,
     'L1_gnn_Wo': 2.915,
     'L1_gnn_bo': 8.0}
    for name, (base, spread) in spreads.items():
        noise = np.random.default_rng([zlib.crc32(name.encode()), seed]).standard_normal(out[name].shape)
        drawn = base * np.exp(spread * noise) if base else spread * noise
        out[name] = jnp.asarray(drawn.astype(out[name].dtype))
    for name, factor in factors.items():
        out[name] = (out[name] * factor).astype(out[name].dtype)
    return out
```

```python
from contextlib import ExitStack

import concourse.bass as bass
from concourse import mybir

F32 = mybir.dt.float32
BF16 = mybir.dt.bfloat16
I32 = mybir.dt.int32
U32 = mybir.dt.uint32
ALU = mybir.AluOpType
ACT = mybir.ActivationFunctionType
AX = mybir.AxisListType

P = 128
N = 6250
E = 200000
D = 256
FE = 128
NB = -(-N // P)
LASTP = N - (NB - 1) * P
CB = 7
NC = NB // CB
CN = CB * P
BT = 8
BE = BT * P
FULL = E // BE
TAILP = (E - FULL * BE) // BT
RING = 3
TILES = (FULL + 1) * BT
G = 256
SBT = 8
SBG = SBT * P // G
NSTEP = -(-(-(-(E + NB * (G - 1)) // G)) // (6 * SBG)) * 6
NG = NSTEP * SBG
NT = NSTEP * SBT
ROWS = NG * G
FILL = ROWS - -(-(ROWS - E) // P) * P
RW = FE + 2
HEADS = 8
HD = D // HEADS
HW = HD + 1
BIG = 1.0e30
NE = 8
DEG = 511
F2 = 512
EPS = 1e-5


class Steps:

    def __init__(self, eng, sem):
        self.eng, self.sem, self.base, self.n = eng, sem, 0, 0

    def add(self, ins):
        ins.then_inc(self.sem, 1)
        self.n += 1

    def wait(self):
        self.eng.wait_ge(self.sem, self.base + self.n)

    def then(self, ins):
        self.add(ins)
        self.wait()

    def enter(self, i, per):
        self.start, self.base, self.n, self.per = self.base + self.n, self.base + self.n + i * per, 0, per

    def leave(self, count):
        assert self.n == self.per, (self.n, self.per)
        self.base, self.n = self.start + count * self.per, 0


class Mem:
    pass


def allocate(nc, ctx):
    m = Mem()

    def sb(name, shape, dt=F32):
        return ctx.enter_context(nc.sbuf_tensor(name, shape, dt))

    m.sb = sb
    m.sem = lambda name: ctx.enter_context(nc.semaphore(name))
    m.bank = [ctx.enter_context(nc.psum_tensor(f"bank{k}", [P, 512], F32)) for k in range(8)]
    m.iota = sb("iota", [P, P])
    m.iota2 = sb("iota2", [P, P])
    m.pidx = sb("pidx", [P, 1])
    m.ident = sb("ident", [P, P])
    m.below = sb("below", [P, P])
    m.above = sb("above", [P, P])
    m.ones = sb("ones", [P, P])
    m.outdeg = sb("outdeg", [P, NB])
    m.indeg = sb("indeg", [P, NB])
    m.blk = sb("blk", [1, NG], I32)
    m.lo = sb("lo", [P, NT])
    m.dst = sb("dst", [P, NT], I32)
    m.r1 = sb("r1", [P, NB * HEADS * HW])
    m.r2 = sb("r2", [P, NB * D])
    m.r3 = sb("r3", [P, 22560])
    return m


def cut(region, at, *dims, dt=None):
    size = 1
    for d in dims:
        size *= d
    words = size // 2 if dt == BF16 else size
    v = region[:, at:at + words]
    assert at + words <= region.shape[1], (at, words, region.shape)
    if dt is not None:
        v = v.bitcast(dt)
    names = "abcd"[:len(dims)]
    if len(dims) > 1:
        v = v.rearrange(f"p ({' '.join(names)}) -> p {' '.join(names)}", **{n: d for n, d in zip(names, dims)})
    return v, at + words


def histogram_and_sort(nc, m, t, edges):
    sem, bank = m.sem, m.bank
    at = 0
    src_i, at = cut(m.r1, at, TILES, dt=I32)
    dst_i, at = cut(m.r1, at, TILES, dt=I32)
    src_lo, at = cut(m.r1, at, TILES)
    src_hi, at = cut(m.r1, at, TILES)
    dst_lo, at = cut(m.r1, at, TILES)
    dst_hi, at = cut(m.r1, at, TILES)
    src_f, at = cut(m.r1, at, TILES)
    dst_f = cut(m.r1, at, TILES)[0]
    LP = 125
    lin, at = cut(m.r2, 0, E // LP, dt=I32)
    lin_f, at = cut(m.r2, at, E // LP)
    pads, at = cut(m.r2, at, 2, RW)
    tmp, at = cut(m.r2, at, BT * P)
    row_hi, at = cut(m.r2, at, RING, BE)
    row_src, at = cut(m.r2, at, RING, BE)
    at = 0
    rec, at = cut(m.r3, at, RING, BT, RW)
    oh_lo, at = cut(m.r3, at, RING, BT, P, dt=BF16)
    oh_hi, at = cut(m.r3, at, RING, BT, 64, dt=BF16)
    od_lo, at = cut(m.r3, at, RING, BT, P, dt=BF16)
    od_hi, at = cut(m.r3, at, RING, BT, 64, dt=BF16)
    hi_rows, at = cut(m.r3, at, RING, BE)
    pos_i, at = cut(m.r3, at, RING, BT, dt=I32)
    rank, at = cut(m.r3, at, RING, BT)
    look, at = cut(m.r3, at, BT)
    hist, at = cut(m.r3, at, 2, P)
    base, at = cut(m.r3, at, P)
    incl, at = cut(m.r3, at, P)
    small, at = cut(m.r3, at, 16)
    small_i, at = cut(m.r3, at, 8, dt=I32)
    giota, at = cut(m.r3, at, NG)
    gcmp, at = cut(m.r3, at, NG)
    zeros, at = cut(m.r3, at, P)
    zb, at = cut(m.r3, at, P, dt=BF16)
    ends_f, at = cut(m.r3, at, 64)
    ends, at = cut(m.r3, at, 64, dt=I32)
    fence, at = cut(m.r3, at, 2)
    H, HD_ = bank[0][0:64, 0:P], bank[1][0:64, 0:P]

    s_fence = sem("place_waits")
    s_pc, s_cst = sem("const_steps"), sem("consts_ready")
    s_mem, s_in, s_lin = sem("pads_set"), sem("indices_loaded"), sem("linear_loaded")
    s_dve, s_hi = sem("sort_vector_steps"), sem("hi_stored")
    s_ohp, s_ohfree, s_h1 = sem("count_onehots_ready"), sem("count_onehots_free"), sem("counts_ready")
    s_bp, s_bm, s_ends, s_pad = sem("base_parts"), sem("base_products"), sem("ends_ready"), sem("pads_stored")
    mult = [(8, FULL * BT)]

    with nc.Block() as block:
        @block.gpsimd
        def _(pool):
            st = Steps(pool, s_pc)
            st.add(pool.iota(m.iota[:, :], [[1, P]], base=0, channel_multiplier=0, allow_small_or_imprecise_dtypes=True))
            st.add(pool.iota(m.iota2[:, :], [[1, P]], base=2, channel_multiplier=0, allow_small_or_imprecise_dtypes=True))
            st.add(pool.iota(m.pidx[:, :], [[0, 1]], base=0, channel_multiplier=1, allow_small_or_imprecise_dtypes=True))
            st.add(pool.iota(giota, [[1, NG]], base=0, channel_multiplier=0, allow_small_or_imprecise_dtypes=True))
            st.add(pool.memset(m.ident[:, :], 0.0))
            st.add(pool.memset(m.ones[:, :], 1.0))
            st.add(pool.memset(zeros, 0.0))
            st.add(pool.memset(zb, 0.0))
            st.add(pool.memset(fence, 0.0))
            st.add(pool.memset(pads, 0.0))
            st.wait()
            st.add(pool.memset(pads[:, :, FE:FE + 1], -1.0))
            st.add(pool.affine_select(out=m.ident[:, :], in_=m.ident[:, :], compare_op=ALU.not_equal, fill=1.0,
                                      base=0, pattern=[[-1, P]], channel_multiplier=1))
            st.add(pool.affine_select(out=m.below[:, :], in_=m.ones[:, :], compare_op=ALU.is_gt, fill=0.0,
                                      base=0, pattern=[[-1, P]], channel_multiplier=1))
            st.add(pool.affine_select(out=m.above[:, :], in_=m.ones[:, :], compare_op=ALU.is_gt, fill=0.0,
                                      base=0, pattern=[[1, P]], channel_multiplier=-1))
            st.wait()
            pool.tensor_copy(fence[0:1, 1:2], fence[0:1, 0:1]).then_inc(s_cst, 1)
            pool.wait_ge(s_cst, 1)
            pool.tensor_tensor(fence[0:1, 1:2], fence[0:1, 0:1], fence[0:1, 0:1], ALU.add).then_inc(s_fence, 1)

        @block.sync
        def _(sp):
            sp.wait_ge(s_mem, 2)
            for dram, into in ((edges["src"], src_i), (edges["dst"], dst_i)):
                sp.dma_start(into[:, 0:FULL * BT].rearrange("p (b t) -> p b t", t=BT),
                             dram[0:FULL * BE].rearrange("(b p t) -> p b t", p=P, t=BT)).then_inc(s_in, 16)
                sp.dma_start(into[0:TAILP, FULL * BT:TILES],
                             dram[FULL * BE:E].rearrange("(p t) -> p t", t=BT)).then_inc(s_in, 16)
            sp.wait_ge(s_cst, 1)
            sp.dma_start(t["sorted"][FILL:ROWS, :].rearrange("(k p) w -> p k w", p=P),
                         pads[:, 0:1, :].to_broadcast([P, (ROWS - FILL) // P, RW])).then_inc(s_pad, 16)
            sp.wait_ge(s_ends, 1)
            sp.wait_ge(s_pad, 16)
            with sp.Fori(0, NB) as b:
                sp.wait_ge(s_pad, b * 16 + 16)
                row = sp.value_load(ends[0:1, bass.ds(b, 1)], min_val=0, max_val=ROWS - G)
                sp.dma_start(t["sorted"][bass.ds(row, G), :].rearrange("(p k) w -> p k w", k=2),
                             pads).then_inc(s_pad, 16)
            sp.wait_ge(s_pad, 16 * (NB + 1))
            sp.wait_ge(s_hi, 16)

        @block.scalar
        def _(act):
            act.dma_start(lin[0:LP, :], edges["src"].rearrange("(p k) -> p k", p=LP)).then_inc(s_lin, 16)
            act.wait_ge(s_dve, 2)
            act.dma_start(t["hi"].rearrange("(p k) -> p k", p=LP), lin_f[0:LP, :]).then_inc(s_hi, 16)

        @block.vector
        def _(dve):
            st = Steps(dve, s_dve)
            v = nc.vector
            v.memset(src_i, -1).then_inc(s_mem, 1)
            v.memset(dst_i, -1).then_inc(s_mem, 1)
            dve.wait_ge(s_lin, 16)
            st.then(v.tensor_scalar(lin[0:LP, :], lin[0:LP, :], 7, None, ALU.arith_shift_right))
            st.then(v.tensor_copy(lin_f[0:LP, :], lin[0:LP, :]))
            dve.wait_ge(s_in, 64)
            st.add(v.tensor_copy(src_f, src_i))
            st.then(v.tensor_copy(dst_f, dst_i))
            for x_i, lo, hi in ((src_i, src_lo, src_hi), (dst_i, dst_lo, dst_hi)):
                as_int = hi.bitcast(I32)
                st.then(v.tensor_scalar(as_int, x_i, 127, None, ALU.bitwise_and))
                st.then(v.tensor_copy(lo, as_int))
                st.then(v.tensor_scalar(as_int, x_i, 7, None, ALU.arith_shift_right))
                st.then(v.tensor_copy(hi, as_int))
            dve.wait_ge(s_cst, 1)
            v.tensor_copy(small[:, 0:1], zeros[:, 0:1]).then_inc(s_ohfree, 2)

            with nc.vector.Fori(0, TILES // BT // 2) as i:
                for r in range(2):
                    col = bass.ds(i * 2 * BT + r * BT, BT)
                    dve.wait_ge(s_ohfree, i * 2 + r + 1)
                    v.tensor_tensor(oh_lo[:, r], m.iota[:, None, :].to_broadcast([P, BT, P]),
                                    src_lo[:, col].unsqueeze(2).to_broadcast([P, BT, P]), ALU.is_equal)
                    v.tensor_tensor(oh_hi[:, r], m.iota[:, None, 0:64].to_broadcast([P, BT, 64]),
                                    src_hi[:, col].unsqueeze(2).to_broadcast([P, BT, 64]), ALU.is_equal).then_inc(s_ohp, 1)
            dve.wait_ge(s_h1, 1)
            st.then(v.tensor_copy(hist[0:64, 0], H))
            st.add(v.tensor_reduce(small[0:64, 1:2], hist[0:64, 0], AX.X, ALU.add))
            st.then(v.tensor_tensor_scan(incl[0:64, :], hist[0:64, 0], zeros[0:64, :], 0.0, ALU.add, ALU.add))
            st.then(v.tensor_scalar(small[0:64, 1:2], small[0:64, 1:2], float(G - 1), None, ALU.add))
            st.then(v.tensor_copy(small_i[0:64, 0:1], small[0:64, 1:2]))
            st.then(v.tensor_scalar(small_i[0:64, 1:2], small_i[0:64, 0:1], 8, 8, ALU.logical_shift_right,
                                    ALU.logical_shift_left))
            st.then(v.tensor_copy(small[0:64, 2:3], small_i[0:64, 1:2]))
            v.tensor_tensor(base[0:64, :], incl[0:64, :], hist[0:64, 0], ALU.subtract).then_inc(s_bp, 1)
            dve.wait_ge(s_bm, 1)
            st.then(v.tensor_copy(small[0:64, 3:4], bank[2][0:64, 0:1]))
            st.add(v.tensor_copy(m.outdeg[:, :], bank[3][:, 0:NB]))
            dve.wait_ge(s_bp, 1)
            st.add(v.tensor_scalar(base[0:64, :], base[0:64, :], small[0:64, 3:4], None, ALU.add))
            st.add(v.tensor_tensor(small[0:64, 4:5], small[0:64, 3:4], small[0:64, 2:3], ALU.add))
            st.then(v.tensor_scalar(small[0:64, 5:6], small[0:64, 3:4], 1.0 / G, None, ALU.mult))
            v.tensor_scalar(gcmp[0:64, :], giota[0:64, :], small[0:64, 5:6], None, ALU.is_ge).then_inc(s_bp, 1)
            dve.wait_ge(s_bm, 2)
            st.add(v.tensor_scalar(m.blk[0:1, 0:NG // 2], bank[4][0:1, 0:NG // 2], -1.0, None, ALU.add))
            st.add(v.tensor_scalar(m.blk[0:1, NG // 2:NG], bank[5][0:1, 0:NG // 2], -1.0, None, ALU.add))
            v.tensor_scalar(ends[0:1, 0:64], bank[6][0:1, 0:64], float(-G), 0.0, ALU.add, ALU.max).then_inc(s_ends, 1)

        @block.tensor
        def _(pe):
            pe.wait_ge(s_cst, 1)
            pe.matmul(H, lhsT=zb[:, 0:64], rhs=zb, start=True, stop=True, skip_group_check=True)
            with nc.tensor.Fori(0, TILES // BT // 2) as i:
                for r in range(2):
                    pe.wait_ge(s_ohp, i * 2 + r + 1)
                    for k in range(BT):
                        mm = pe.matmul(H, lhsT=oh_hi[:, r, k, :], rhs=oh_lo[:, r, k, :], start=False, stop=True,
                                       skip_group_check=True)
                    mm.then_inc(s_ohfree, 1)
            pe.wait_ge(s_ohfree, TILES // BT + 2)
            pe.transpose(bank[7][:, 0:64], m.ones[0:64, :], m.ident[0:64, 0:64]).then_inc(s_h1, 1)
            pe.wait_ge(s_bp, 1)
            pe.matmul(bank[2][0:64, 0:1], lhsT=m.above[0:64, 0:64], rhs=small[0:64, 2:3], start=True, stop=True)
            pe.transpose(bank[3][:, 0:64], hist[0:64, 0], m.ident[0:64, 0:64]).then_inc(s_bm, 1)
            pe.wait_ge(s_bp, 2)
            for h in range(2):
                pe.matmul(bank[4 + h][0:1, 0:NG // 2], lhsT=m.ones[0:NB, 0:1], rhs=gcmp[0:NB, h * NG // 2:(h + 1) * NG // 2],
                          start=True, stop=True)
            pe.matmul(bank[6][0:1, 0:64], lhsT=small[0:64, 4:5], rhs=m.ident[0:64, 0:64], start=True,
                      stop=True).then_inc(s_bm, 1)

    s_rec = [sem(f"edges_loaded{r}") for r in range(RING)]
    s_sc = [sem(f"rows_stored{r}") for r in range(RING)]
    s_read = sem("rows_read")
    s_oh, s_look, s_pos = sem("onehots_ready"), sem("lookups_done"), sem("places_ready")
    s_hu, s_hc, s_dh, s_dv, s_fin = (sem(x) for x in ("count_updates", "count_copies", "dst_counts",
                                                      "places_steps", "indeg_turned"))
    attr_v = edges["edge_attr_128"]

    with nc.Block() as block:
        @block.sync
        def _(sp):
            def load(b, r, part=P):
                first, count = b * BE, part * BT
                rows = bass.ds(first, count)
                sp.dma_start(rec[0:part, r, :, 0:FE], attr_v[rows, :].rearrange("(p t) f -> p t f", t=BT)).then_inc(s_rec[r], 16)
                sp.dma_start(row_hi[0:64, r, 0:count], t["hi"][rows].unsqueeze(0).to_broadcast([64, count])).then_inc(s_rec[r], 16)
                sp.dma_start(row_src[:, r, 0:count].bitcast(I32),
                             edges["src"][rows].unsqueeze(0).to_broadcast([P, count])).then_inc(s_rec[r], 16)
            for r in range(RING):
                load(r, r)
            with sp.Fori(1, FULL // RING) as i:
                for r in range(RING):
                    sp.wait_ge(s_sc[r], i * 16 * BT)
                    load(i * RING + r, r)
            sp.wait_ge(s_sc[0], 16 * BT * (FULL // RING))
            load(FULL, 0, TAILP)
            for r in range(RING):
                sp.wait_ge(s_sc[r], 16 * BT * (FULL // RING + (r == 0)))

        @block.vector
        def _(dve):
            v = nc.vector
            v.tensor_copy(small[:, 0:1], zeros[:, 0:1]).then_inc(s_pos, 1)
            st = Steps(dve, s_dv)

            def onehots_and_ranks(b, i, r, part=P):
                w = part * BT
                col = bass.ds(b * BT, BT)
                dve.wait_ge(s_rec[r], i * 48 + 48)
                v.tensor_scalar(hi_rows[0:64, r, 0:w], row_hi[0:64, r, 0:w], m.pidx[0:64, :], None, ALU.is_equal)
                st.add(v.tensor_tensor(oh_lo[:, r], m.iota[:, None, :].to_broadcast([P, BT, P]),
                                       src_lo[:, col].unsqueeze(2).to_broadcast([P, BT, P]), ALU.is_equal))
                v.tensor_tensor(oh_hi[:, r], m.iota[:, None, 0:64].to_broadcast([P, BT, 64]),
                                src_hi[:, col].unsqueeze(2).to_broadcast([P, BT, 64]), ALU.is_equal).then_inc(s_oh, 1)
                rows = row_src[:, r, 0:w].bitcast(I32).rearrange("p (e t) -> p t e", t=BT)
                cols = [src_f[:, bass.ds(b * BT + k, 1)] for k in range(BT)]
                for k in range(BT):
                    v.scalar_tensor_tensor(out=tmp[0:part, k * P:k * P + part], in0=rows[0:part, k, :], scalar=cols[k][0:part, :],
                                           in1=m.below[0:part, 0:part], op0=ALU.is_equal, op1=ALU.mult,
                                           accum_out=rank[0:part, r, k:k + 1])
                v.tensor_copy(rec[0:part, r, :, FE], src_lo[0:part, col])
                st.add(v.tensor_copy(rec[0:part, r, :, FE + 1], dst_f[0:part, col]))
                v.tensor_tensor(od_lo[:, r], m.iota[:, None, :].to_broadcast([P, BT, P]),
                                dst_lo[:, col].unsqueeze(2).to_broadcast([P, BT, P]), ALU.is_equal)
                v.tensor_tensor(od_hi[:, r], m.iota[:, None, 0:64].to_broadcast([P, BT, 64]),
                                dst_hi[:, col].unsqueeze(2).to_broadcast([P, BT, 64]), ALU.is_equal).then_inc(s_oh, 1)

            def places(b, r, part=P):
                for h in range(2):
                    half = slice(h * BT // 2, (h + 1) * BT // 2)
                    dve.wait_ge(s_look, b * 2 + h + 1)
                    if h == 0:
                        st.wait()
                    lk = bank[2 + h][0:part, :].rearrange("p (t n) -> p t n", n=P)
                    tv = tmp[0:part, :].rearrange("p (t n) -> p t n", n=P)[:, half]
                    st.then(v.tensor_tensor(tv, lk, oh_lo[0:part, r, half], ALU.mult))
                    st.then(v.tensor_reduce(look[0:part, half], tv, AX.X, ALU.add))
                v.tensor_tensor(pos_i[0:part, r], look[0:part, :], rank[0:part, r], ALU.add).then_inc(s_pos, 1)

            onehots_and_ranks(0, 0, 0)
            st.wait()
            with nc.vector.Fori(0, FULL // RING - 1) as i:
                st.enter(i, 6 * RING)
                for r in range(RING):
                    onehots_and_ranks(i * RING + r + 1, i + (r + 1) // RING, (r + 1) % RING)
                    places(i * RING + r, r)
                st.leave(FULL // RING - 1)
            for b in range(FULL - RING, FULL):
                onehots_and_ranks(b + 1, (b + 1) // RING, (b + 1) % RING, P if b + 1 < FULL else TAILP)
                places(b, b % RING)
            places(FULL, FULL % RING, TAILP)
            dve.wait_ge(s_dh, FULL + 1)
            st.then(v.tensor_copy(hist[0:64, 0], HD_))
            dve.wait_ge(s_hu, 1)
            v.tensor_copy(small[:, 0:1], zeros[:, 0:1]).then_inc(s_fin, 1)
            dve.wait_ge(s_fin, 2)
            v.tensor_copy(m.indeg[:, :], bank[4][:, 0:NB])

        @block.tensor
        def _(pe):
            pe.matmul(H, lhsT=m.ident[0:64, 0:64], rhs=base[0:64, :], start=True, stop=True,
                      skip_group_check=True).then_inc(s_hu, 1)
            pe.matmul(HD_, lhsT=zb[:, 0:64], rhs=zb, start=True, stop=True, skip_group_check=True)

            def batch(b, r, part=P):
                pe.wait_ge(s_oh, b * 2 + 1)
                pe.wait_ge(s_pos, b + 1)
                rows = hi_rows[0:64, r, 0:part * BT].rearrange("p (e t) -> p t e", t=BT)
                for k in range(BT):
                    pe.wait_ge(s_hc, b * BT + k + 1)
                    mm = pe.matmul(bank[2 + k // 4][0:part, (k % 4) * P:(k % 4 + 1) * P], lhsT=rows[:, k, :],
                                   rhs=hist[0:64, k % 2], start=True, stop=True, skip_group_check=True)
                    if k % 4 == 3:
                        mm.then_inc(s_look, 1)
                    pe.matmul(H, lhsT=oh_hi[:, r, k, :], rhs=oh_lo[:, r, k, :], start=False, stop=True,
                              skip_group_check=True).then_inc(s_hu, 1)
                pe.wait_ge(s_oh, b * 2 + 2)
                for k in range(BT):
                    mm = pe.matmul(HD_, lhsT=od_hi[:, r, k, :], rhs=od_lo[:, r, k, :], start=False, stop=True,
                                   skip_group_check=True)
                mm.then_inc(s_dh, 1)

            with nc.tensor.Fori(0, FULL // RING) as i:
                for r in range(RING):
                    batch(i * RING + r, r)
            batch(FULL, 0, TAILP)
            pe.wait_ge(s_fin, 1)
            pe.transpose(bank[4][:, 0:64], hist[0:64, 0], m.ident[0:64, 0:64]).then_inc(s_fin, 1)

        @block.scalar
        def _(act):
            with nc.scalar.Fori(0, FULL + 1) as b:
                for k in range(BT):
                    act.wait_ge(s_hu, b * BT + k + 1)
                    nc.scalar.activation(hist[0:64, k % 2], H, ACT.Copy).then_inc(s_hc, 1)

        @block.gpsimd
        def _(pool):
            def batch(b, r, part=P):
                pool.wait_ge(s_pos, b + 2)
                pool.wait_ge(s_fence, b + 1)
                pool.tensor_tensor(fence[0:1, 1:2], fence[0:1, 0:1], fence[0:1, 0:1], ALU.add).then_inc(s_fence, 1)
                for k in range(BT):
                    pool.indirect_dma_start(
                        out=t["sorted"][:, :], out_offset=bass.IndirectOffsetOnAxis(ap=pos_i[0:part, r, k:k + 1], axis=0),
                        in_=rec[0:part, r, k, :], in_offset=None).then_inc(s_sc[r], 16)
            with nc.gpsimd.Fori(0, FULL // RING) as i:
                for r in range(RING):
                    batch(i * RING + r, r)
            batch(FULL, 0, TAILP)


def load_blocks(nc, eng, m, step):
    return list(nc.values_load_multi_w_load_instructions(
        m.blk[0:1, bass.ds(step * SBG, SBG)], engines=(eng.engine,), min_val=0, max_val=NB - 1)[1])


def edge_sums(nc, m, t):
    sem, bank = m.sem, m.bank
    sums = m.r1[:, 0:NB * FE]
    at = 0
    rows, at = cut(m.r3, at, 2, SBG, 2, RW)
    onehot, at = cut(m.r3, at, 2, SBT, P)
    s_ld, s_free = [sem(f"sorted_loaded{r}") for r in range(2)], sem("sorted_free")
    s_oh, s_mm, s_st, s_z = sem("sum_onehots"), sem("sum_products"), sem("sum_steps"), sem("sums_zeroed")

    with nc.Block() as block:
        @block.sync
        def _(sp):
            def load(s, r):
                sp.dma_start(rows[:, r], t["sorted"][bass.ds(s * SBT * P, SBT * P), :].rearrange(
                    "(g p j) w -> p g (j w)", p=P, j=2).rearrange("p g (j w) -> p g j w", j=2)).then_inc(s_ld[r], 16)
            load(0, 0)
            load(1, 1)
            with sp.Fori(1, NSTEP // 2) as i:
                for r in range(2):
                    sp.wait_ge(s_mm, i * 2 + r - 1)
                    load(i * 2 + r, r)

        @block.vector
        def _(dve):
            v = nc.vector
            st = Steps(dve, s_st)
            st.then(v.memset(sums, 0.0))

            def build(s, i, r):
                dve.wait_ge(s_ld[r], i * 16 + 16)
                words = rows[:, r].rearrange("p g j w -> p (g j) w")
                v.tensor_scalar(m.lo[:, bass.ds(s * SBT, SBT)], words[:, :, FE], 2.0, None, ALU.add)
                v.tensor_copy(m.dst[:, bass.ds(s * SBT, SBT)], words[:, :, FE + 1])
                v.tensor_tensor(onehot[:, r], m.iota[:, None, :].to_broadcast([P, SBT, P]),
                                words[:, :, FE:FE + 1].to_broadcast([P, SBT, P]), ALU.is_equal).then_inc(s_oh, 1)

            def add(s, r):
                blocks = load_blocks(nc, dve, m, s)
                dve.wait_ge(s_mm, s + 1)
                for g in range(SBG):
                    to = sums[:, bass.ds(blocks[g] * FE, FE)]
                    st.then(v.tensor_tensor(to, to, bank[4 * r + g][:, 0:FE], ALU.add))

            build(0, 0, 0)
            with nc.vector.Fori(0, NSTEP // 2 - 1) as i:
                st.enter(i, 2 * SBG)
                build(i * 2 + 1, i, 1)
                add(i * 2, 0)
                build(i * 2 + 2, i + 1, 0)
                add(i * 2 + 1, 1)
                st.leave(NSTEP // 2 - 1)
            build(NSTEP - 1, NSTEP // 2 - 1, 1)
            add(NSTEP - 2, 0)
            add(NSTEP - 1, 1)

        @block.tensor
        def _(pe):
            def products(s, r):
                pe.wait_ge(s_oh, s + 1)
                for g in range(SBG):
                    for j in range(2):
                        mm = pe.matmul(bank[4 * r + g][:, 0:FE], lhsT=onehot[:, r, 2 * g + j, :],
                                       rhs=rows[:, r, g, j, 0:FE], start=(j == 0), stop=(j == 1))
                mm.then_inc(s_mm, 1)

            products(0, 0)
            products(1, 1)
            with nc.tensor.Fori(1, NSTEP // 2) as i:
                for r in range(2):
                    pe.wait_ge(s_st, (i * 2 + r - 1) * SBG + 1)
                    products(i * 2 + r, r)



def put(dma, sem, amount=16):
    dma.then_inc(sem, amount)


def row_norm(dve, act_sem, back_sem, st, v, m, x, out, stats, mv, rstd, want_act, want_back):
    for b in range(CB):
        st.add(v.bn_stats(stats[:, b, :], x[:, b, :]))
    st.wait()
    st.add(v.tensor_copy(rstd[:, 0, 0:1], stats[:, 0, 0:1]))
    for b in range(CB):
        ins = v.bn_aggr(mv[:, b, :], stats[:, b, :])
    ins.then_inc(act_sem, 1)
    dve.wait_ge(back_sem, want_back)
    st.then(v.reciprocal(rstd[:, 1, :], rstd[:, 0, :]))
    for b in range(CB):
        st.add(v.tensor_scalar(out[:, b, :], x[:, b, :], mv[:, b, 0:1], rstd[:, 1, b:b + 1], ALU.subtract, ALU.mult))
    st.wait()


ROW_NORM_STEPS = 2 * CB + 2


def node_stage(nc, m, t, w):
    sem, bank = m.sem, m.bank
    sums = m.r1[:, 0:NB * FE]
    w1, at = cut(m.r1, NB * FE, 2, NE, D)
    wqkv, at = cut(m.r1, at, 2, 3, D)
    wsum, at = cut(m.r1, at, D)
    b1, at = cut(m.r1, at, 2 * NE)
    router, at = cut(m.r1, at, 2, NE)
    w2, at = cut(m.r3, 0, 2, NE, D)
    xs, at = cut(m.r3, at, CB, D)
    tok, at = cut(m.r3, at, CB, D)
    zin, at_out = cut(m.r3, at, CB, D)
    zout, _ = cut(m.r3, at_out, CB, D)
    kvo, at = cut(m.r3, at, CB, 2 * D)
    emb, at = cut(m.r3, at, CB, D)
    tT, at = cut(m.r3, at, 2 * CN)
    hT, at = cut(m.r3, at, 2, 2, CN)
    rowc, at = cut(m.r3, at, 6, D)
    bkv, at = cut(m.r3, at, 2 * D)
    b2, at = cut(m.r3, at, D)
    combT, at = cut(m.r3, at, CN)
    nodes, at = cut(m.r3, at, 2, NB)
    bn, at = cut(m.r3, at, CB, 6)
    mv, at = cut(m.r3, at, CB, 2)
    rstd, at = cut(m.r3, at, 2, CB)
    zidx, at = cut(m.r3, at, 2, CB, dt=I32)
    lg, at = cut(m.r3, at, CB, NE)
    top, at = cut(m.r3, at, CB, NE)
    topi, at = cut(m.r3, at, CB, NE, dt=U32)
    topf, at = cut(m.r3, at, CB, NE)
    wts, at = cut(m.r3, at, 3, CB)
    comb, at = cut(m.r3, at, CB, NE)
    comb2, at = cut(m.r3, at, CB, NE)
    eps, at = cut(m.r3, at, 2)
    fences, at = cut(m.r3, at, 4)
    SCALE = float(HD) ** -0.5
    names = ("node_weights", "node_setup", "x_loaded", "node_setup_steps", "degrees_clipped", "z_rows", "norm_stats",
             "norm_deviation", "cent_ready", "cent_done", "sums_copied", "sums_turned", "sums_turned_copied",
             "sums_projected", "tokens_ready", "tokens_turned", "tokens_copied", "logits_ready", "gap_ready",
             "gap_exp", "combine_ready", "combine_turned", "combine_copied", "bias_ready", "hidden_products",
             "hidden_ready", "expert_products", "expert_added", "x2_ready", "qkv_products", "qkv_read",
             "node_steps", "x2_kv_stored", "kv_ready", "z_fence", "bias_added")
    s = {n: sem(n) for n in names}
    NW = 16

    with nc.Block() as block:
        @block.sync
        def _(sp):
            loads = [
                (w1, w["L0_ffn_w1"].rearrange("e (k p) f -> p k e f", p=P)),
                (w2, w["L0_ffn_w2"].rearrange("e (k p) f -> p k e f", p=P)),
                (wqkv[:, :, 0], w["L1_gnn_Wq"].rearrange("(k p) f -> p k f", p=P)),
                (wqkv[:, :, 1], w["L1_gnn_Wk"].rearrange("(k p) f -> p k f", p=P)),
                (wqkv[:, :, 2], w["L1_gnn_Wv"].rearrange("(k p) f -> p k f", p=P)),
                (wsum, w["L0_gnn_W_sum"]),
                (rowc[:, 0], w["L0_gnn_W_cent"].to_broadcast([P, D])),
                (rowc[:, 1], w["L0_gnn_b_cent"].unsqueeze(0).to_broadcast([P, D])),
                (rowc[:, 2], w["L0_gnn_W_vor"].to_broadcast([P, D])),
                (rowc[:, 3], w["L0_gnn_b_vor"].unsqueeze(0).to_broadcast([P, D])),
                (rowc[:, 4], w["L0_gnn_b_sum"].unsqueeze(0).to_broadcast([P, D])),
                (rowc[:, 5], w["L1_gnn_bq"].unsqueeze(0).to_broadcast([P, D])),
                (bkv[:, 0:D], w["L1_gnn_bk"].unsqueeze(0).to_broadcast([P, D])),
                (bkv[:, D:2 * D], w["L1_gnn_bv"].unsqueeze(0).to_broadcast([P, D])),
                (b2[0:NE, :], w["L0_ffn_b2"]),
            ]
            for dst, src in loads[0:2]:
                for k in range(2):
                    put(sp.dma_start(dst[:, k], src[:, k]), s["node_weights"])
            for dst, src in loads[2:]:
                put(sp.dma_start(dst, src), s["node_weights"])
            for e in range(NE):
                put(sp.dma_start(b1[:, 2 * e:2 * e + 2], w["L0_ffn_b1"][e, :].rearrange("(k p) -> p k", p=P),
                                 allow_slow_non_contiguous=True), s["node_weights"])
            for k in range(2):
                put(sp.dma_start(router[:, k, :], w["L0_ffn_router_w"][:, k * P:(k + 1) * P].rearrange("e p -> p e"),
                                 allow_slow_non_contiguous=True), s["node_weights"])
            sp.wait_ge(s["node_setup"], 1)
            for k, name in enumerate(("node_vec1_n2", "node_vec1")):
                put(sp.dma_start(nodes[:, k, 0:NB - 1], w[name][0:(NB - 1) * P, :].rearrange("(b p) o -> p (b o)", p=P),
                                 allow_slow_non_contiguous=True), s["node_weights"])
                put(sp.dma_start(nodes[0:LASTP, k, NB - 1:NB], w[name][(NB - 1) * P:N, :]), s["node_weights"])

            def chunk(c, last=False, first=False):
                if not first:
                    sp.wait_ge(s["x2_kv_stored"], c * 32)
                if last:
                    put(sp.dma_start(xs[:, 0:CB - 1], w["x"][c * CN:c * CN + (CB - 1) * P, :].rearrange(
                        "(b p) d -> p b d", p=P)), s["x_loaded"])
                    put(sp.dma_start(xs[0:LASTP, CB - 1], w["x"][N - LASTP:N, :]), s["x_loaded"])
                else:
                    put(sp.dma_start(xs, w["x"][bass.ds(c * CN, CN), :].rearrange("(b p) d -> p b d", p=P)),
                        s["x_loaded"])
                sp.wait_ge(s["x2_ready"], c + 1)
                put(sp.dma_start(t["x2"][bass.ds(c * CN, CN), :].rearrange("(b p) d -> p b d", p=P), xs),
                    s["x2_kv_stored"])
                sp.wait_ge(s["kv_ready"], c + 1)
                put(sp.dma_start(t["kv"][bass.ds(c * CN, CN), :].rearrange("(b p) d -> p b d", p=P), kvo),
                    s["x2_kv_stored"])

            chunk(0, first=True)
            with sp.Fori(1, NC - 1) as c:
                chunk(c)
            chunk(NC - 1, last=True)
            sp.wait_ge(s["x2_kv_stored"], NC * 32)

        LOADS = 16 * (4 + 13 + NE + 2 + 4)

        @block.gpsimd
        def _(pool):
            pool.memset(fences[:, 0:2], 0.0).then_inc(s["z_fence"], 1)
            pool.wait_ge(s["z_fence"], 1)
            with nc.gpsimd.Fori(0, NC) as c:
                pool.wait_ge(s["degrees_clipped"], c + 1)
                pool.wait_ge(s["z_fence"], c + 1)
                pool.tensor_tensor(fences[0:1, 1:2], fences[0:1, 0:1], fences[0:1, 0:1], ALU.add).then_inc(s["z_fence"], 1)
                for k, (table, z) in enumerate(((w["L0_gnn_z_in"], zin), (w["L0_gnn_z_out"], zout))):
                    for b in range(CB):
                        pool.indirect_dma_start(out=z[:, b, :], out_offset=None, in_=table[:, :],
                                                in_offset=bass.IndirectOffsetOnAxis(ap=zidx[:, k, b:b + 1], axis=0)
                                                ).then_inc(s["z_rows"], 16)

        @block.vector
        def _(dve):
            v = nc.vector
            pre = Steps(dve, s["node_setup_steps"])
            v.memset(nodes, 0.0).then_inc(s["node_setup"], 1)
            pre.then(v.memset(eps, EPS))
            dve.wait_ge(s["node_weights"], LOADS)
            pre.then(v.tensor_scalar(rowc[:, 5], rowc[:, 5], SCALE, None, ALU.mult))
            st = Steps(dve, s["node_steps"])

            def chunk(c):
                cols = bass.ds(c * CB, CB)
                dve.wait_ge(s["x_loaded"], c * 16 + 16)
                if isinstance(c, int):
                    dve.wait_ge(s["x_loaded"], c * 16 + 32)
                v.tensor_scalar(zidx[:, 0], m.indeg[:, cols], float(DEG), None, ALU.min)
                v.tensor_scalar(zidx[:, 1], m.outdeg[:, cols], float(DEG), None, ALU.min).then_inc(s["degrees_clipped"], 1)
                row_norm(dve, s["norm_stats"], s["norm_deviation"], st, v, m, xs, tok, bn, mv, rstd, None, c * 3 + 1)
                st.then(v.tensor_tensor(xs, xs, tok, ALU.add))
                for b in range(CB):
                    st.add(v.scalar_tensor_tensor(out=emb[:, b, :], in0=rowc[:, 0], scalar=nodes[:, 0, bass.ds(c * CB + b, 1)],
                                                  in1=rowc[:, 1], op0=ALU.mult, op1=ALU.add))
                    ins = v.scalar_tensor_tensor(out=tok[:, b, :], in0=rowc[:, 2], scalar=nodes[:, 1, bass.ds(c * CB + b, 1)],
                                                 in1=rowc[:, 3], op0=ALU.mult, op1=ALU.add)
                ins.then_inc(s["cent_ready"], 1)
                v.tensor_copy(hT[:, 0, 0, :], sums[:, bass.ds(c * CN, CN)]).then_inc(s["sums_copied"], 1)
                for b in range(CB):
                    st.add(v.scalar_tensor_tensor(out=xs[:, b, :], in0=rowc[:, 4], scalar=m.outdeg[:, bass.ds(c * CB + b, 1)],
                                                  in1=xs[:, b, :], op0=ALU.mult, op1=ALU.add))
                st.wait()
                dve.wait_ge(s["cent_done"], c + 1)
                st.then(v.tensor_tensor(xs, xs, emb, ALU.add))
                st.then(v.tensor_tensor(xs, xs, tok, ALU.add))
                dve.wait_ge(s["z_rows"], (c + 1) * (2 * CB * 16))
                st.then(v.tensor_tensor(xs, xs, zin, ALU.add))
                st.then(v.tensor_tensor(xs, xs, zout, ALU.add))
                dve.wait_ge(s["sums_projected"], c + 1)
                for k in range(4):
                    e = min(2 * k + 2, CB)
                    part = xs[:, 2 * k:e, :].rearrange("p b d -> p (b d)")
                    st.add(v.tensor_tensor(part, part, bank[2 + k][:, 0:(e - 2 * k) * D], ALU.add))
                st.wait()
                row_norm(dve, s["norm_stats"], s["norm_deviation"], st, v, m, xs, tok, bn, mv, rstd, None, c * 3 + 2)
                v.tensor_copy(rstd[:, 0, 0:1], mv[:, 0, 0:1]).then_inc(s["tokens_ready"], 1)
                st.then(v.tensor_tensor(xs, xs, tok, ALU.add))
                dve.wait_ge(s["logits_ready"], c + 1)
                st.then(v.tensor_copy(lg, bank[4][:, 0:CB * NE].rearrange("p (b e) -> p b e", e=NE)))
                st.add(v.tensor_copy(fences[:, 2:3], lg[:, 0, 0:1]))
                for b in range(CB):
                    st.add(v.max(top[:, b, :], lg[:, b, :]))
                st.wait()
                v.tensor_tensor(wts[:, 0], top[:, :, 1], top[:, :, 0], ALU.subtract).then_inc(s["gap_ready"], 1)
                for b in range(CB):
                    st.add(v.max_index(topi[:, b, :], top[:, b, :], lg[:, b, :]))
                st.wait()
                st.add(v.tensor_copy(topf, topi))
                dve.wait_ge(s["gap_exp"], c + 1)
                st.then(v.tensor_scalar(wts[:, 2], wts[:, 1], 1.0, None, ALU.add))
                st.then(v.reciprocal(wts[:, 2], wts[:, 2]))
                st.then(v.tensor_tensor(wts[:, 1], wts[:, 1], wts[:, 2], ALU.mult))
                st.add(v.tensor_tensor(comb, m.iota[:, None, 0:NE].to_broadcast([P, CB, NE]),
                                       topf[:, :, 0:1].to_broadcast([P, CB, NE]), ALU.is_equal))
                st.then(v.tensor_tensor(comb2, m.iota[:, None, 0:NE].to_broadcast([P, CB, NE]),
                                        topf[:, :, 1:2].to_broadcast([P, CB, NE]), ALU.is_equal))
                st.add(v.tensor_tensor(comb, comb, wts[:, 2].unsqueeze(2).to_broadcast([P, CB, NE]), ALU.mult))
                st.then(v.tensor_tensor(comb2, comb2, wts[:, 1].unsqueeze(2).to_broadcast([P, CB, NE]), ALU.mult))
                st.then(v.tensor_tensor(comb, comb, comb2, ALU.add))
                v.tensor_copy(fences[:, 3:4], comb[:, 0, 0:1]).then_inc(s["combine_ready"], 1)
                dve.wait_ge(s["bias_ready"], c + 1)
                for k in range(4):
                    e = min(2 * k + 2, CB)
                    part = xs[:, 2 * k:e, :].rearrange("p b d -> p (b d)")
                    st.add(v.tensor_tensor(part, part, bank[4 + k][:, 0:(e - 2 * k) * D], ALU.add))
                st.wait()
                v.tensor_copy(fences[:, 2:3], comb[:, 0, 0:1]).then_inc(s["bias_added"], 1)
                for e in range(NE):
                    dve.wait_ge(s["expert_products"], c * NE + e + 1)
                    for b in range(CB):
                        ins = v.scalar_tensor_tensor(out=xs[:, b, :], in0=bank[4 + b // 2][:, (b % 2) * D:(b % 2 + 1) * D],
                                                     scalar=comb[:, b, e:e + 1], in1=xs[:, b, :], op0=ALU.mult, op1=ALU.add)
                    ins.then_inc(s["expert_added"], 1)
                    dve.wait_ge(s["expert_added"], c * NE + e + 1)
                v.tensor_copy(rstd[:, 0, 0:1], xs[:, 0, 0:1]).then_inc(s["x2_ready"], 1)
                dve.wait_ge(s["x2_ready"], c + 1)
                row_norm(dve, s["norm_stats"], s["norm_deviation"], st, v, m, xs, tok, bn, mv, rstd, None, c * 3 + 3)
                v.tensor_copy(rstd[:, 0, 0:1], mv[:, 0, 0:1]).then_inc(s["tokens_ready"], 1)
                for b in range(CB):
                    dve.wait_ge(s["qkv_products"], c * CB + b + 1)
                    v.scalar_tensor_tensor(out=m.r2[:, bass.ds(c * CB * D + b * D, D)], in0=bank[3 + b % 3][:, 0:D],
                                           scalar=SCALE, in1=rowc[:, 5], op0=ALU.mult, op1=ALU.add)
                    v.tensor_tensor(kvo[:, b, :], bank[b % 3][:, 0:2 * D], bkv, ALU.add).then_inc(s["qkv_read"], 1)
                dve.wait_ge(s["qkv_read"], c * CB + CB)
                v.tensor_copy(fences[:, 3:4], comb[:, 0, 0:1]).then_inc(s["kv_ready"], 1)

            with nc.vector.Fori(0, NC - 1) as c:
                st.enter(c, NODE_STEPS)
                chunk(c)
                st.leave(NC - 1)
            chunk(NC - 1)

        @block.tensor
        def _(pe):
            pe.wait_ge(s["node_weights"], LOADS)

            def turn(c, which):
                pe.wait_ge(s["tokens_ready"], c * 2 + which + 1)
                for k in range(2):
                    for b in range(CB):
                        q = k * CB + b
                        tr = pe.transpose(bank[q // 4][:, (q % 4) * P:(q % 4 + 1) * P], tok[:, b, k * P:(k + 1) * P],
                                          m.ident[:, :])
                tr.then_inc(s["tokens_turned"], 1)

            def hidden(c, e):
                if e > 0:
                    pe.wait_ge(s["hidden_ready"], c * NE + e)
                for f in range(2):
                    for h in range(2):
                        for k in range(2):
                            mm = pe.matmul(bank[2 * f + h][:, 0:CN // 2], lhsT=w1[:, k, e, f * P:(f + 1) * P],
                                           rhs=tT[:, k * CN + h * CN // 2:k * CN + (h + 1) * CN // 2],
                                           start=(k == 0), stop=(k == 1))
                mm.then_inc(s["hidden_products"], 1)

            def expert(c, e):
                pe.wait_ge(s["hidden_ready"], c * NE + e + 1)
                if e > 0:
                    pe.wait_ge(s["expert_added"], c * NE + e)
                else:
                    pe.wait_ge(s["bias_added"], c + 1)
                for b in range(CB):
                    for k in range(2):
                        mm = pe.matmul(bank[4 + b // 2][:, (b % 2) * D:(b % 2 + 1) * D], lhsT=hT[:, e % 2, k, b * P:(b + 1) * P],
                                       rhs=w2[:, k, e, :], start=(k == 0), stop=(k == 1))
                mm.then_inc(s["expert_products"], 1)

            with nc.tensor.Fori(0, NC) as c:
                pe.wait_ge(s["sums_copied"], c + 1)
                for b in range(CB):
                    tr = pe.transpose(bank[b // 4][:, (b % 4) * P:(b % 4 + 1) * P], hT[:, 0, 0, b * P:(b + 1) * P],
                                      m.ident[:, :])
                tr.then_inc(s["sums_turned"], 1)
                pe.wait_ge(s["sums_turned_copied"], c + 1)
                for b in range(CB):
                    mm = pe.matmul(bank[2 + b // 2][:, (b % 2) * D:(b % 2 + 1) * D], lhsT=hT[:, 0, 1, b * P:(b + 1) * P],
                                   rhs=wsum, start=True, stop=True)
                mm.then_inc(s["sums_projected"], 1)
                turn(c, 0)
                pe.wait_ge(s["tokens_copied"], c * 2 + 1)
                for b in range(CB):
                    for k in range(2):
                        mm = pe.matmul(bank[4][:, b * NE:(b + 1) * NE], lhsT=tT[:, k * CN + b * P:k * CN + (b + 1) * P],
                                       rhs=router[:, k, :], start=(k == 0), stop=(k == 1))
                mm.then_inc(s["logits_ready"], 1)
                hidden(c, 0)
                pe.wait_ge(s["combine_ready"], c + 1)
                for b in range(CB):
                    tr = pe.transpose(bank[5 + b // 4][0:NE, (b % 4) * P:(b % 4 + 1) * P], comb[:, b, :], m.ident[:, :])
                tr.then_inc(s["combine_turned"], 1)
                pe.wait_ge(s["combine_copied"], c + 1)
                for b in range(CB):
                    mm = pe.matmul(bank[4 + b // 2][:, (b % 2) * D:(b % 2 + 1) * D], lhsT=combT[0:NE, b * P:(b + 1) * P],
                                   rhs=b2[0:NE, :], start=True, stop=True)
                mm.then_inc(s["bias_ready"], 1)
                for e in range(NE):
                    if e + 1 < NE:
                        hidden(c, e + 1)
                    expert(c, e)
                turn(c, 1)
                pe.wait_ge(s["tokens_copied"], c * 2 + 2)
                for b in range(CB):
                    if b >= 3:
                        pe.wait_ge(s["qkv_read"], c * CB + b - 2)
                    for k in range(2):
                        pe.matmul(bank[3 + b % 3][:, 0:D], lhsT=tT[:, k * CN + b * P:k * CN + (b + 1) * P],
                                  rhs=wqkv[:, k, 0, :], start=(k == 0), stop=(k == 1))
                    for k in range(2):
                        mm = pe.matmul(bank[b % 3][:, 0:2 * D], lhsT=tT[:, k * CN + b * P:k * CN + (b + 1) * P],
                                       rhs=wqkv[:, k, 1:3, :].rearrange("p a d -> p (a d)"), start=(k == 0), stop=(k == 1))
                    mm.then_inc(s["qkv_products"], 1)

        @block.scalar
        def _(act):
            a = nc.scalar.activation
            act.wait_ge(s["node_setup_steps"], 1)
            act.wait_ge(s["node_weights"], LOADS)

            def deviation(c, which):
                act.wait_ge(s["norm_stats"], c * 3 + which + 1)
                a(rstd[:, 0, :], mv[:, :, 1], ACT.Sqrt, bias=eps[:, 0:1]).then_inc(s["norm_deviation"], 1)

            def copy_turned(c, which):
                act.wait_ge(s["tokens_turned"], c * 2 + which + 1)
                for q in range(4):
                    n = min(512, 2 * CN - 512 * q)
                    ins = a(tT[:, 512 * q:512 * q + n], bank[q][:, 0:n], ACT.Copy)
                ins.then_inc(s["tokens_copied"], 1)

            with nc.scalar.Fori(0, NC) as c:
                deviation(c, 0)
                act.wait_ge(s["cent_ready"], c + 1)
                a(emb, emb, ACT.Sigmoid)
                a(tok, tok, ACT.Sigmoid).then_inc(s["cent_done"], 1)
                act.wait_ge(s["sums_turned"], c + 1)
                a(hT[:, 0, 1, 0:512], bank[0][:, :], ACT.Copy)
                a(hT[:, 0, 1, 512:CN], bank[1][:, 0:CN - 512], ACT.Copy).then_inc(s["sums_turned_copied"], 1)
                deviation(c, 1)
                copy_turned(c, 0)
                act.wait_ge(s["gap_ready"], c + 1)
                a(wts[:, 1], wts[:, 0], ACT.Exp).then_inc(s["gap_exp"], 1)
                act.wait_ge(s["combine_turned"], c + 1)
                a(combT[0:NE, 0:512], bank[5][0:NE, :], ACT.Copy)
                a(combT[0:NE, 512:CN], bank[6][0:NE, 0:CN - 512], ACT.Copy).then_inc(s["combine_copied"], 1)
                for e in range(NE):
                    act.wait_ge(s["hidden_products"], c * NE + e + 1)
                    if e >= 2:
                        act.wait_ge(s["expert_products"], c * NE + e - 1)
                    for f in range(2):
                        for h in range(2):
                            ins = a(hT[:, e % 2, f, h * CN // 2:(h + 1) * CN // 2], bank[2 * f + h][:, 0:CN // 2],
                                    ACT.Gelu, bias=b1[:, 2 * e + f:2 * e + f + 1])
                    ins.then_inc(s["hidden_ready"], 1)
                deviation(c, 2)
                copy_turned(c, 1)


NODE_STEPS = 3 * ROW_NORM_STEPS + 1 + CB + CB + 4 + 4 + 1 + 2 + CB + CB + 1 + 3 + 2 + 2 + 1 + 4


class At:

    def __init__(self, i, k, half=0):
        self.i, self.k = i, k
        self.r, self.use, self.s, self.half = k % 3, i + k // 3, i * 3 + k, half % 2

    def plus(self, d):
        return At(self.i, self.k + d, self.half + d)


def attention(nc, m, t):
    sem, bank = m.sem, m.bank
    acc = m.r1[:, :].rearrange("p (b h w) -> p b h w", h=HEADS, w=HW)
    q_all = m.r2
    kv, at = cut(m.r3, 0, 3, SBT, 2 * D)
    onehot, at = cut(m.r3, at, 3, SBT, P)
    turned, at = cut(m.r3, at, 2, SBT * P)
    pv, at = cut(m.r3, at, SBT, HEADS * HW)
    prod, at = cut(m.r3, at, 2, 2, D)
    score, at = cut(m.r3, at, 2, SBT, HEADS)
    reset, at = cut(m.r3, at, 2, SBT, HEADS)
    sT, at = cut(m.r3, at, P)
    fwd, at = cut(m.r3, at, P)
    ends, at = cut(m.r3, at, SBT, HEADS + 1)
    edge, at = cut(m.r3, at, 3, 2, SBT)
    idx, at = cut(m.r3, at, 3, SBT, dt=I32)
    tmax, at = cut(m.r3, at, SBT, HEADS)
    some, at = cut(m.r3, at, SBT)
    gmax, at = cut(m.r3, at, SBG, HEADS)
    newmax, at = cut(m.r3, at, SBG, HEADS)
    drop, at = cut(m.r3, at, SBG, HEADS)
    alpha, at = cut(m.r3, at, SBG, HEADS)
    diff, at = cut(m.r3, at, SBT, HEADS)
    run, at = cut(m.r3, at, NB * HEADS)
    prev, at = cut(m.r3, at, P)
    nxt, at = cut(m.r3, at, P)
    fence, at = cut(m.r3, at, 4)
    names = ("attention_setup", "shift_ready", "index_ready", "onehot_ready", "neighbours_ready", "onehot_turned",
             "onehot_copied", "q_selected", "scores_grouped", "score_ready", "scores_turned", "scores_copied",
             "maxima_scanned", "maxima_back", "node_ends_ready", "tile_maxima", "maxima_ready", "maxima_edges",
             "diff_ready", "alpha_ready", "weights_ready", "values_ready", "sums_ready", "sums_added",
             "score_steps", "update_steps", "gather_fence")
    s = {n: sem("a_" + n) for n in names}
    s_g = [sem(f"kv_gathered{r}") for r in range(3)]
    KA, KB = 2 * SBG, 4 + 5 * SBG

    with nc.Block() as block:
        @block.gpsimd
        def _(pool):
            st = Steps(pool, s["shift_ready"])
            st.add(pool.memset(prev, 0.0))
            st.add(pool.memset(nxt, 0.0))
            st.then(pool.memset(fence[:, 0:1], 0.0))
            st.add(pool.affine_select(out=prev, in_=prev, compare_op=ALU.not_equal, fill=1.0, base=-1,
                                      pattern=[[1, P]], channel_multiplier=-1))
            st.add(pool.affine_select(out=nxt, in_=nxt, compare_op=ALU.not_equal, fill=1.0, base=-1,
                                      pattern=[[-1, P]], channel_multiplier=1))
            st.wait()
            pool.tensor_tensor(fence[0:1, 1:2], fence[0:1, 0:1], fence[0:1, 0:1], ALU.add).then_inc(s["gather_fence"], 1)

            def gather(a, free=True):
                if free:
                    pool.wait_ge(s["values_ready"], a.s - 2)
                pool.wait_ge(s["index_ready"], a.s + 1)
                pool.wait_ge(s["gather_fence"], a.s + 1)
                pool.tensor_tensor(fence[0:1, 1:2], fence[0:1, 0:1], fence[0:1, 0:1], ALU.add).then_inc(s["gather_fence"], 1)
                for k in range(SBT):
                    pool.indirect_dma_start(out=kv[:, a.r, k, :], out_offset=None, in_=t["kv"][:, :],
                                            in_offset=bass.IndirectOffsetOnAxis(ap=idx[:, a.r, k:k + 1], axis=0)
                                            ).then_inc(s_g[a.r], 16)
            for k in range(3):
                gather(At(0, k), free=False)
            with nc.gpsimd.Fori(1, NSTEP // 3) as i:
                for k in range(3):
                    gather(At(i, k))

        @block.vector
        def _(dve):
            v = nc.vector
            v.memset(m.r1[:, :], 0.0)
            v.memset(run, -BIG)
            for whole in (score, reset, fwd):
                v.memset(whole, 0.0)
            dve.wait_ge(s["shift_ready"], 3)
            v.memset(fence[:, 2:3], 0.0).then_inc(s["attention_setup"], 1)
            dve.wait_ge(s["attention_setup"], 1)
            sa, sb = Steps(dve, s["score_steps"]), Steps(dve, s["update_steps"])

            def index(a):
                v.tensor_copy(idx[:, a.r], m.dst[:, bass.ds(a.s * SBT, SBT)]).then_inc(s["index_ready"], 1)

            def build(a):
                lo = m.lo[:, bass.ds(a.s * SBT, SBT)]
                v.tensor_tensor(onehot[:, a.r], m.iota2[:, None, :].to_broadcast([P, SBT, P]),
                                lo.unsqueeze(2).to_broadcast([P, SBT, P]), ALU.is_equal).then_inc(s["onehot_ready"], 1)
                dve.wait_ge(s["neighbours_ready"], a.s + 1)
                near = bank[7][:, 3 * P:3 * P + 2 * SBT].rearrange("p (a t) -> p a t", a=2)
                for k in range(2):
                    ins = v.tensor_tensor(edge[:, a.r, k], near[:, k], lo, ALU.not_equal)
                return ins

            def scores(a, g):
                if g == 0:
                    dve.wait_ge(s_g[a.r], a.use * 16 * SBT + 16 * SBT)
                dve.wait_ge(s["q_selected"], a.s * SBG + g + 1)
                sa.then(v.tensor_tensor(prod[:, g % 2], bank[2 + g % 2][:, :].rearrange("p (t d) -> p t d", d=D),
                                        kv[:, a.r, 2 * g:2 * g + 2, 0:D], ALU.mult))
                sa.add(v.tensor_reduce(score[:, a.half, 2 * g:2 * g + 2, :].rearrange("p t h -> p (t h)"),
                                       prod[:, g % 2].rearrange("p t (h d) -> p (t h) d", d=HD), AX.X, ALU.add))
                if g == SBG - 1:
                    v.tensor_scalar(reset[:, a.half], edge[:, a.r, 0].unsqueeze(2).to_broadcast([P, SBT, HEADS]),
                                    -BIG, None, ALU.mult).then_inc(s["score_ready"], 1)

            def body(a, new=True, old=True):
                b = a.plus(-1) if old else None
                if new:
                    sa.base, sa.n = a.s * KA, 0
                if old:
                    sb.base, sb.n = b.s * KB, 0
                    dve.wait_ge(s["scores_copied"], b.s + 1)
                    rows = slice(64 * b.half, 64 * b.half + 64)
                    v.tensor_tensor_scan(fwd[rows, :], bank[6][rows, P:2 * P], sT[rows, :], -BIG, ALU.add,
                                         ALU.max).then_inc(s["maxima_scanned"], 1)
                    blocks = load_blocks(nc, dve, m, b.s)
                if new:
                    scores(a, 0)
                if old:
                    last = edge[:, b.r, 1]
                    dve.wait_ge(s["maxima_back"], b.s + 1)
                    sb.add(v.tensor_tensor(ends[:, :, 0:HEADS], bank[7][:, 64 * b.half:64 * b.half + 64].rearrange("p (t h) -> p t h", h=HEADS),
                                           last.unsqueeze(2).to_broadcast([P, SBT, HEADS]), ALU.mult))
                    v.tensor_copy(ends[:, :, HEADS], last).then_inc(s["node_ends_ready"], 1)
                if new:
                    scores(a, 1)
                if old:
                    dve.wait_ge(s["tile_maxima"], b.s + 1)
                    tm = bank[7][:, P:P + SBT * (HEADS + 1)].rearrange("p (t h) -> p t h", h=HEADS + 1)
                    sb.then(v.tensor_scalar(some, tm[:, :, HEADS], 1.0, BIG, ALU.subtract, ALU.mult))
                    sb.then(v.tensor_tensor(tmax, tm[:, :, 0:HEADS], some.unsqueeze(2).to_broadcast([P, SBT, HEADS]), ALU.add))
                    pair = tmax.rearrange("p (g j) h -> p g j h", j=2)
                    sb.then(v.tensor_tensor(gmax, pair[:, :, 0], pair[:, :, 1], ALU.max))
                    for g in range(SBG):
                        own = run[:, bass.ds(blocks[g] * HEADS, HEADS)]
                        sb.then(v.tensor_tensor(newmax[:, g], own, gmax[:, g], ALU.max))
                        sb.then(v.tensor_tensor(drop[:, g], own, newmax[:, g], ALU.subtract))
                        sb.then(v.tensor_tensor(own, newmax[:, g], newmax[:, g], ALU.max))
                    v.tensor_copy(fence[:, 3:4], newmax[:, 0, 0:1]).then_inc(s["maxima_ready"], 1)
                if new:
                    scores(a, 2)
                if old:
                    dve.wait_ge(s["maxima_edges"], b.s + 1)
                    v.tensor_tensor(diff, score[:, b.half], bank[7][:, 2 * P - 56:2 * P + 8].rearrange("p (t h) -> p t h", h=HEADS),
                                    ALU.subtract).then_inc(s["diff_ready"], 1)
                if new:
                    scores(a, 3)
                if old:
                    dve.wait_ge(s["weights_ready"], b.s + 1)
                    pvh = pv.rearrange("p t (h w) -> p t h w", w=HW)
                    v.tensor_tensor(pvh[:, :, :, 0:HD], kv[:, b.r, :, D:2 * D].rearrange("p t (h d) -> p t h d", d=HD),
                                    pvh[:, :, :, HD:HW].to_broadcast([P, SBT, HEADS, HD]), ALU.mult
                                    ).then_inc(s["values_ready"], 1)
                if new:
                    if a.more:
                        index(a.plus(2))
                    if a.next:
                        build(a.plus(1)).then_inc(s["attention_setup"], 1)
                        dve.wait_ge(s["attention_setup"], a.s + 3)
                if old:
                    for g in range(SBG):
                        own = m.r1[:, bass.ds(blocks[g] * (HEADS * HW), HEADS * HW)]
                        ownh = own.rearrange("p (h w) -> p h w", w=HW)
                        if g == 0:
                            dve.wait_ge(s["alpha_ready"], b.s + 1)
                        sb.then(v.tensor_tensor(ownh, ownh, alpha[:, g].unsqueeze(2).to_broadcast([P, HEADS, HW]), ALU.mult))
                        dve.wait_ge(s["sums_ready"], b.s * SBG + g + 1)
                        sb.then(v.tensor_tensor(own, own, bank[4 + g % 2][:, 0:HEADS * HW], ALU.add))

            def run_at(a, **kw):
                body(a, **kw)

            index(At(0, 0))
            index(At(0, 1))
            build(At(0, 0)).then_inc(s["attention_setup"], 1)
            dve.wait_ge(s["attention_setup"], 2)
            steps_program(nc.vector, run_at)

        @block.tensor
        def _(pe):
            pe.wait_ge(s["shift_ready"], 5)
            pe.wait_ge(s["attention_setup"], 1)

            def turn(a):
                pe.wait_ge(s["onehot_ready"], a.s + 1)
                lo = m.lo[:, bass.ds(a.s * SBT, SBT)]
                pe.matmul(bank[7][:, 3 * P:3 * P + SBT], lhsT=prev, rhs=lo, start=True, stop=True, skip_group_check=True)
                pe.matmul(bank[7][:, 3 * P + SBT:3 * P + 2 * SBT], lhsT=nxt, rhs=lo, start=True, stop=True,
                          skip_group_check=True).then_inc(s["neighbours_ready"], 1)
                for k in range(SBT):
                    tr = pe.transpose(bank[k // 4][:, (k % 4) * P:(k % 4 + 1) * P], onehot[:, a.r, k, :], m.ident[:, :])
                    if k % 4 == 3:
                        tr.then_inc(s["onehot_turned"], 1)

            def select(a, g, blk):
                if g == 0:
                    pe.wait_ge(s["onehot_copied"], a.s * 2 + 2)
                if g >= 2:
                    pe.wait_ge(s["score_steps"], a.s * KA + 2 * (g - 2) + 1)
                for j in range(2):
                    mm = pe.matmul(bank[2 + g % 2][:, j * D:(j + 1) * D],
                                   lhsT=turned[:, a.half, (2 * g + j) * P:(2 * g + j + 1) * P],
                                   rhs=q_all[:, bass.ds(blk * D, D)], start=True, stop=True, skip_group_check=True)
                mm.then_inc(s["q_selected"], 1)

            def body(a, new=True, old=True):
                b = a.plus(-1) if old else None
                if new:
                    blocks = load_blocks(nc, pe, m, a.s)
                    select(a, 0, blocks[0])
                    select(a, 1, blocks[1])
                if old:
                    pe.wait_ge(s["maxima_scanned"], b.s + 1)
                    pe.transpose(bank[7][:, 0:P], fwd, m.ident[:, :]).then_inc(s["maxima_back"], 1)
                    pe.wait_ge(s["node_ends_ready"], b.s + 1)
                    for k in range(SBT):
                        mm = pe.matmul(bank[7][:, P + k * (HEADS + 1):P + (k + 1) * (HEADS + 1)],
                                       lhsT=onehot[:, b.r, k, :], rhs=ends[:, k, :], start=True, stop=True,
                                       skip_group_check=True)
                    mm.then_inc(s["tile_maxima"], 1)
                if new:
                    select(a, 2, blocks[2])
                if old:
                    pe.wait_ge(s["maxima_ready"], b.s + 1)
                    for k in range(SBT):
                        mm = pe.matmul(bank[7][:, 2 * P - 56 + k * HEADS:2 * P - 56 + (k + 1) * HEADS],
                                       lhsT=turned[:, b.half, k * P:(k + 1) * P], rhs=newmax[:, k // 2, :], start=True,
                                       stop=True, skip_group_check=True)
                    mm.then_inc(s["maxima_edges"], 1)
                if new:
                    select(a, 3, blocks[3])
                    pe.wait_ge(s["score_ready"], a.s + 1)
                    pe.transpose(bank[6][:, 0:P], score.rearrange("p a t h -> p (a t h)"), m.ident[:, :])
                    pe.transpose(bank[6][:, P:2 * P], reset.rearrange("p a t h -> p (a t h)"), m.ident[:, :]).then_inc(s["scores_turned"], 1)
                for g in range(SBG):
                    if g == 2 and new and a.next:
                        turn(a.plus(1))
                    if old:
                        if g == 0:
                            pe.wait_ge(s["values_ready"], b.s + 1)
                        if g >= 2:
                            pe.wait_ge(s["update_steps"], b.s * KB + KB - 2 * SBG + 2 * (g - 2) + 2)
                        for j in range(2):
                            mm = pe.matmul(bank[4 + g % 2][:, 0:HEADS * HW], lhsT=onehot[:, b.r, 2 * g + j, :],
                                           rhs=pv[:, 2 * g + j, :], start=(j == 0), stop=(j == 1))
                        mm.then_inc(s["sums_ready"], 1)

            turn(At(0, 0))
            steps_program(nc.tensor, body)

        @block.scalar
        def _(act):
            a_ = nc.scalar.activation

            def copy_onehots(a):
                for h in range(2):
                    act.wait_ge(s["onehot_turned"], a.s * 2 + h + 1)
                    a_(turned[:, a.half, h * 512:(h + 1) * 512], bank[h][:, :], ACT.Copy).then_inc(s["onehot_copied"], 1)

            def body(a, new=True, old=True):
                b = a.plus(-1) if old else None
                if old:
                    act.wait_ge(s["maxima_ready"], b.s + 1)
                    a_(alpha, drop, ACT.Exp).then_inc(s["alpha_ready"], 1)
                    act.wait_ge(s["diff_ready"], b.s + 1)
                    a_(pv.rearrange("p t (h w) -> p t h w", w=HW)[:, :, :, HD], diff, ACT.Exp).then_inc(s["weights_ready"], 1)
                if new:
                    act.wait_ge(s["scores_turned"], a.s + 1)
                    rows = slice(64 * a.half, 64 * a.half + 64)
                    a_(sT[rows, :], bank[6][rows, 0:P], ACT.Copy).then_inc(s["scores_copied"], 1)
                    if a.next:
                        copy_onehots(a.plus(1))

            copy_onehots(At(0, 0))
            steps_program(nc.scalar, body)


def steps_program(engine, body):
    def at(i, k, half, more=True, nxt=True):
        a = At(i, k, half)
        a.more, a.next = more, nxt
        return a
    body(at(0, 0, 0), old=False)
    loops = (NSTEP - 4) // 6
    with engine.Fori(0, loops) as i:
        two = i * 2
        for k in range(1, 7):
            body(at(two, k, k % 2))
    for step in range(1 + 6 * loops, NSTEP):
        body(at(0, step, step % 2, more=step + 2 < NSTEP, nxt=step + 1 < NSTEP))
    body(at(0, NSTEP, NSTEP % 2), new=False)


def output_stage(nc, m, t, w, out):
    sem, bank = m.sem, m.bank
    x3 = m.r2
    tT_all, at = cut(m.r3, 0, NC, 2 * CN)
    x2, at = cut(m.r3, at, CB, D)
    att, at = cut(m.r3, at, CB, D)
    aT, at = cut(m.r3, at, 2 * CN)
    tok, at = cut(m.r3, at, CB, D)
    at0 = at
    wo, at = cut(m.r3, at, 2, D)
    bo, at = cut(m.r3, at, D)
    bn, at = cut(m.r3, at, CB, 6)
    mv, at = cut(m.r3, at, CB, 2)
    rstd, at = cut(m.r3, at, 2, CB)
    den, at = cut(m.r3, at, CB, HEADS)
    eps, at = cut(m.r3, at, 2)
    fences, at = cut(m.r3, at, 4)
    valid, at = cut(m.r3, at, NB)
    msum, at = cut(m.r3, at, 2)
    keep, at = cut(m.r3, at, NB, 2)
    wr, at = cut(m.r3, at, 2, NE)
    br, at = cut(m.r3, at, NE)
    rt, at = cut(m.r3, at, 12, NE)
    rti, at = cut(m.r3, at, NE, dt=U32)
    acc = m.r1[:, :]
    names = ("output_weights", "valid_ready", "o_setup", "x2_loaded", "attended", "att_turned", "att_copied",
             "att_projected", "o_steps", "o_norm_stats", "o_norm_deviation", "o_tokens_ready", "o_turned", "o_copied",
             "feature_sums", "route_products", "route_exp", "route_steps", "chosen", "expert_weights",
             "mean_ready", "weights_row", "weights_col", "scaled", "f_hidden", "f_gelu", "f_products",
             "f_steps", "f_norm_stats", "f_norm_deviation", "y_ready", "y_stored", "f_rows")
    s = {n: sem(n) for n in names}

    with nc.Block() as block:
        @block.gpsimd
        def _(pool):
            st = Steps(pool, s["valid_ready"])
            st.then(pool.memset(valid, 1.0))
            st.add(pool.affine_select(out=valid[:, NB - 1:NB], in_=valid[:, NB - 1:NB], compare_op=ALU.is_gt, fill=0.0,
                                      base=LASTP, pattern=[[0, 1]], channel_multiplier=-1))

        @block.sync
        def _(sp):
            loads = [(wo, w["L1_gnn_Wo"].rearrange("(k p) f -> p k f", p=P)),
                     (bo, w["L1_gnn_bo"].unsqueeze(0).to_broadcast([P, D])),
                     (wr, w["L1_ffn_Wr"].rearrange("(k p) f -> p k f", p=P)),
                     (br[0:1, :], w["L1_ffn_br"].unsqueeze(0))]
            for dst, src in loads:
                sp.dma_start(dst, src).then_inc(s["output_weights"], 16)

            def load(c):
                sp.dma_start(x2, t["x2"][bass.ds(c * CN, CN), :].rearrange("(b p) d -> p b d", p=P)).then_inc(s["x2_loaded"], 16)
            load(0)
            with sp.Fori(1, NC) as c:
                sp.wait_ge(s["o_tokens_ready"], c)
                load(c)

        @block.vector
        def _(dve):
            v = nc.vector
            v.memset(eps, EPS).then_inc(s["o_setup"], 1)
            v.memset(msum, 0.0).then_inc(s["o_setup"], 1)
            dve.wait_ge(s["output_weights"], 64)
            dve.wait_ge(s["o_setup"], 2)
            st = Steps(dve, s["o_steps"])
            with nc.vector.Fori(0, NC) as c:
                st.enter(c, 3 + 4 + CB + ROW_NORM_STEPS + 3)
                own = acc[:, bass.ds(c * (CB * HEADS * HW), CB * HEADS * HW)].rearrange("p (b w) -> p b w", w=HW)
                denf = den.rearrange("p b h -> p (b h)")
                st.then(v.tensor_scalar(denf, own[:, :, HD], 1e-30, None, ALU.max))
                st.then(v.reciprocal(denf, denf))
                v.tensor_tensor(att.rearrange("p b (h d) -> p (b h) d", d=HD), own[:, :, 0:HD],
                                denf.unsqueeze(2).to_broadcast([P, CB * HEADS, HD]), ALU.mult).then_inc(s["attended"], 1)
                dve.wait_ge(s["x2_loaded"], c * 16 + 16)
                for b in range(CB):
                    st.add(v.tensor_tensor(x2[:, b, :], x2[:, b, :], bo, ALU.add))
                st.wait()
                dve.wait_ge(s["att_projected"], c + 1)
                for k in range(4):
                    e = min(2 * k + 2, CB)
                    part = x2[:, 2 * k:e, :].rearrange("p b d -> p (b d)")
                    st.add(v.tensor_tensor(part, part, bank[4 + k][:, 0:(e - 2 * k) * D], ALU.add))
                st.wait()
                st.add(v.tensor_copy(x3[:, bass.ds(c * CB * D, CB * D)], x2.rearrange("p b d -> p (b d)")))
                row_norm(dve, s["o_norm_stats"], s["o_norm_deviation"], st, v, m, x2, tok, bn, mv, rstd, None, c + 1)
                kp = keep[:, bass.ds(c * CB, CB), :]
                st.add(v.tensor_copy(kp[:, :, 0], mv[:, :, 0]))
                st.add(v.tensor_copy(kp[:, :, 1], rstd[:, 1, :]))
                v.tensor_copy(fences[:, 0:1], mv[:, 0, 0:1]).then_inc(s["o_tokens_ready"], 1)
                dve.wait_ge(s["feature_sums"], c + 1)
                st.add(v.tensor_tensor(msum, msum, bank[4][:, 0:2], ALU.add))
            st.leave(NC)
            st.wait()
            r = Steps(dve, s["route_steps"])
            r.then(v.tensor_scalar(msum, msum, 1.0 / N, None, ALU.mult))
            v.tensor_copy(fences[:, 1:2], msum[:, 0:1]).then_inc(s["mean_ready"], 1)
            dve.wait_ge(s["route_products"], 1)
            one = lambda k, a=0, b=NE: rt[0:1, k, a:b]
            r.then(v.tensor_tensor(one(0), bank[7][0:1, 0:NE], br[0:1, :], ALU.add))
            cap = float(-(-int(N * 1.25) // NE) if (N * 1.25) == int(N * 1.25) else int(N * 1.25 / NE) + 1)
            exps = [0]

            def softmax(src, dst, n):
                r.then(v.tensor_reduce(one(10, 0, 1), one(src, 0, n), AX.X, ALU.max))
                v.tensor_scalar(one(11, 0, n), one(src, 0, n), one(10, 0, 1), None, ALU.subtract).then_inc(s["chosen"], 1)
                exps[0] += 1
                dve.wait_ge(s["route_exp"], exps[0])
                r.then(v.tensor_reduce(one(10, 1, 2), one(dst, 0, n), AX.X, ALU.add))
                r.then(v.reciprocal(one(10, 2, 3), one(10, 1, 2)))
                r.then(v.tensor_scalar(one(dst, 0, n), one(dst, 0, n), one(10, 2, 3), None, ALU.mult))

            softmax(0, 1, NE)
            r.then(v.tensor_scalar(one(2), one(1), float(N), None, ALU.mult))
            r.add(v.tensor_scalar(one(3), one(2), cap, None, ALU.is_gt))
            r.then(v.tensor_scalar(one(4), one(2), 1.0, None, ALU.max))
            r.then(v.reciprocal(one(4), one(4)))
            r.then(v.tensor_scalar(one(4), one(4), cap, -1.0, ALU.mult, ALU.add))
            r.then(v.tensor_tensor(one(4), one(4), one(3), ALU.mult))
            r.then(v.tensor_scalar(one(4), one(4), 1.0, None, ALU.add))
            r.then(v.tensor_tensor(one(5), one(1), one(4), ALU.mult))
            softmax(5, 6, NE)
            r.then(v.max(one(7), one(6)))
            r.then(v.max_index(rti[0:1, :], one(7), one(6)))
            softmax(7, 8, 2)
            v.tensor_copy(one(9), one(8)).then_inc(s["weights_row"], 1)

        @block.scalar
        def _(act):
            a = nc.scalar.activation
            act.wait_ge(s["o_setup"], 1)
            with nc.scalar.Fori(0, NC) as c:
                act.wait_ge(s["att_turned"], c + 1)
                for q in range(4):
                    n = min(512, 2 * CN - 512 * q)
                    ins = a(aT[:, 512 * q:512 * q + n], bank[q][:, 0:n], ACT.Copy)
                ins.then_inc(s["att_copied"], 1)
                act.wait_ge(s["o_norm_stats"], c + 1)
                a(rstd[:, 0, :], mv[:, :, 1], ACT.Sqrt, bias=eps[:, 0:1]).then_inc(s["o_norm_deviation"], 1)
                act.wait_ge(s["o_turned"], c + 1)
                a(aT[:, 0:512], bank[0][:, :], ACT.Copy)
                for q in range(1, 4):
                    n = min(512, 2 * CN - 512 * q)
                    ins = a(aT[:, 512 * q:512 * q + n], bank[q][:, 0:n], ACT.Copy)
                ins.then_inc(s["f_rows"], 1)
                act.wait_ge(s["f_rows"], c + 1)
                a(fences[:, 2:3], aT[:, 0:1], ACT.Copy)
                a(tT_all[:, bass.ds(c, 1), :].rearrange("p o n -> p (o n)"), aT, ACT.Copy).then_inc(s["o_copied"], 1)
            for k in range(3):
                act.wait_ge(s["chosen"], k + 1)
                n, dst = ((NE, 1), (NE, 6), (2, 8))[k]
                a(rt[0:1, dst, 0:n], rt[0:1, 11, 0:n], ACT.Exp).then_inc(s["route_exp"], 1)

        @block.tensor
        def _(pe):
            pe.wait_ge(s["output_weights"], 64)
            pe.wait_ge(s["valid_ready"], 2)
            with nc.tensor.Fori(0, NC) as c:
                def turn(src, ready):
                    pe.wait_ge(ready, c + 1)
                    for k in range(2):
                        for b in range(CB):
                            q = k * CB + b
                            tr = pe.transpose(bank[q // 4][:, (q % 4) * P:(q % 4 + 1) * P], src[:, b, k * P:(k + 1) * P],
                                              m.ident[:, :])
                    return tr
                turn(att, s["attended"]).then_inc(s["att_turned"], 1)
                pe.wait_ge(s["att_copied"], c + 1)
                for b in range(CB):
                    for k in range(2):
                        mm = pe.matmul(bank[4 + b // 2][:, (b % 2) * D:(b % 2 + 1) * D],
                                       lhsT=aT[:, k * CN + b * P:k * CN + (b + 1) * P], rhs=wo[:, k, :],
                                       start=(k == 0), stop=(k == 1))
                mm.then_inc(s["att_projected"], 1)
                turn(tok, s["o_tokens_ready"]).then_inc(s["o_turned"], 1)
                for k in range(2):
                    for b in range(CB):
                        mm = pe.matmul(bank[4][:, k:k + 1], lhsT=tok[:, b, k * P:(k + 1) * P],
                                       rhs=valid[:, bass.ds(c * CB + b, 1)], start=(b == 0), stop=(b == CB - 1))
                mm.then_inc(s["feature_sums"], 1)
                pe.wait_ge(s["o_copied"], c + 1)
            pe.wait_ge(s["mean_ready"], 1)
            for k in range(2):
                mm = pe.matmul(bank[7][0:1, 0:NE], lhsT=msum[:, k:k + 1], rhs=wr[:, k, :], start=(k == 0), stop=(k == 1))
            mm.then_inc(s["route_products"], 1)

    w1, at1 = cut(m.r1, 0, 2, 2, F2)
    w2, at1 = cut(m.r1, at1, 2, 4, D)
    hT, at1 = cut(m.r1, at1, 2, CN)
    y, at1 = cut(m.r1, at1, CB, D)
    b1, at1 = cut(m.r1, at1, 2, 4)
    b2, at1 = cut(m.r1, at1, 2, D)
    gamma, at1 = cut(m.r1, at1, D)
    beta, at1 = cut(m.r1, at1, D)
    share, at1 = cut(m.r1, at1, 2)
    b2s, at1 = cut(m.r1, at1, D)
    wrow, at1 = cut(m.r1, at1, 2, P)

    with nc.Block() as block:
        @block.sync
        def _(sp):
            for e in range(2):
                x = sp.value_load(rti[0:1, e:e + 1], min_val=0, max_val=NE - 1)
                sp.dma_start(w1[:, e], w["L1_ffn_W1"][bass.ds(x, 1), :, :].rearrange("o (k p) f -> p (o k) f", p=P)
                             ).then_inc(s["expert_weights"], 16)
                sp.dma_start(w2[:, e], w["L1_ffn_W2"][bass.ds(x, 1), :, :].rearrange("o (k p) f -> p (o k) f", p=P)
                             ).then_inc(s["expert_weights"], 16)
                sp.dma_start(b1[:, e], w["L1_ffn_b1"][bass.ds(x, 1), :].rearrange("o (k p) -> p (o k)", p=P),
                             allow_slow_non_contiguous=True).then_inc(s["expert_weights"], 16)
                sp.dma_start(b2[0:1, e], w["L1_ffn_b2"][bass.ds(x, 1), :]).then_inc(s["expert_weights"], 16)
            for dst, name in ((gamma, "L1_ffn_gamma"), (beta, "L1_ffn_beta")):
                sp.dma_start(dst, w[name].unsqueeze(0).to_broadcast([P, D])).then_inc(s["expert_weights"], 16)

            with sp.Fori(0, NC - 1) as c:
                sp.wait_ge(s["y_ready"], c + 1)
                sp.dma_start(out[bass.ds(c * CN, CN), :].rearrange("(b p) d -> p b d", p=P), y).then_inc(s["y_stored"], 16)
            sp.wait_ge(s["y_ready"], NC)
            c = NC - 1
            sp.dma_start(out[c * CN:c * CN + (CB - 1) * P, :].rearrange("(b p) d -> p b d", p=P),
                         y[:, 0:CB - 1]).then_inc(s["y_stored"], 16)
            sp.dma_start(out[N - LASTP:N, :], y[0:LASTP, CB - 1]).then_inc(s["y_stored"], 16)
            sp.wait_ge(s["y_stored"], 16 * (NC + 1))

        @block.vector
        def _(dve):
            v = nc.vector
            for e in range(2):
                ins = v.tensor_scalar(wrow[0:1, e], m.ones[0:1, :], rt[0:1, 9, e:e + 1], None, ALU.mult)
            ins.then_inc(s["weights_row"], 1)
            dve.wait_ge(s["weights_col"], 1)
            v.tensor_copy(share, bank[7][:, 0:2]).then_inc(s["scaled"], 1)
            dve.wait_ge(s["scaled"], 1)
            dve.wait_ge(s["expert_weights"], 160)
            for e in range(2):
                v.tensor_scalar(w2[:, e], w2[:, e], share[:, e:e + 1], None, ALU.mult)
            dve.wait_ge(s["weights_col"], 2)
            v.tensor_copy(b2s, bank[6][:, 0:D]).then_inc(s["scaled"], 1)
            dve.wait_ge(s["scaled"], 2)
            st = Steps(dve, s["f_steps"])

            def chunk(c, first=False):
                xc = x3[:, bass.ds(c * CB * D, CB * D)].rearrange("p (b d) -> p b d", d=D)
                kp = keep[:, bass.ds(c * CB, CB), :]
                st.then(v.tensor_copy(mv, kp))
                for b in range(CB):
                    st.add(v.tensor_scalar(tok[:, b, :], xc[:, b, :], mv[:, b, 0:1], mv[:, b, 1:2], ALU.subtract, ALU.mult))
                st.wait()
                for b in range(CB):
                    st.add(v.tensor_tensor(tok[:, b, :], tok[:, b, :], b2s, ALU.add))
                st.wait()
                dve.wait_ge(s["f_products"], c + 1)
                for k in range(4):
                    e = min(2 * k + 2, CB)
                    part = tok[:, 2 * k:e, :].rearrange("p b d -> p (b d)")
                    st.add(v.tensor_tensor(part, part, bank[4 + k][:, 0:(e - 2 * k) * D], ALU.add))
                st.wait()
                row_norm(dve, s["f_norm_stats"], s["f_norm_deviation"], st, v, m, tok, att, bn, mv, rstd, None, c + 1)
                st.then(v.tensor_tensor(att, att, gamma.unsqueeze(1).to_broadcast([P, CB, D]), ALU.mult))
                st.then(v.tensor_tensor(att, att, beta.unsqueeze(1).to_broadcast([P, CB, D]), ALU.add))
                if not first:
                    dve.wait_ge(s["y_stored"], c * 16)
                v.tensor_tensor(y, att, xc, ALU.add).then_inc(s["y_ready"], 1)

            chunk(0, first=True)
            st.base, st.n = st.n, 0
            with nc.vector.Fori(1, NC) as c:
                st.start, st.base, st.n = 0, c * (1 + 2 * CB + 4 + ROW_NORM_STEPS + 2), 0
                chunk(c)

        @block.scalar
        def _(act):
            a = nc.scalar.activation
            act.wait_ge(s["expert_weights"], 160)
            with nc.scalar.Fori(0, NC) as c:
                for ef in range(8):
                    act.wait_ge(s["f_hidden"], c * 8 + ef + 1)
                    if ef >= 2:
                        act.wait_ge(s["f_rows"], NC + c * 8 + ef - 1)
                    for h in range(2):
                        ins = a(hT[:, ef % 2, h * CN // 2:(h + 1) * CN // 2], bank[2 * (ef % 2) + h][:, 0:CN // 2], ACT.Gelu,
                                bias=b1[:, ef // 4, ef % 4:ef % 4 + 1])
                    ins.then_inc(s["f_gelu"], 1)
                act.wait_ge(s["f_norm_stats"], c + 1)
                a(rstd[:, 0, :], mv[:, :, 1], ACT.Sqrt, bias=eps[:, 0:1]).then_inc(s["f_norm_deviation"], 1)

        @block.tensor
        def _(pe):
            pe.wait_ge(s["weights_row"], 2)
            for e in range(2):
                mm = pe.matmul(bank[7][:, e:e + 1], lhsT=wrow[0:1, e], rhs=m.ones[0:1, 0:1], start=True, stop=True,
                               skip_group_check=True)
            mm.then_inc(s["weights_col"], 1)
            pe.wait_ge(s["expert_weights"], 160)
            for e in range(2):
                mm = pe.matmul(bank[6][:, 0:D], lhsT=wrow[0:1, e], rhs=b2[0:1, e], start=(e == 0), stop=(e == 1))
            mm.then_inc(s["weights_col"], 1)
            pe.wait_ge(s["scaled"], 2)

            def hidden(c, ef):
                if ef >= 2:
                    pe.wait_ge(s["f_gelu"], c * 8 + ef - 1)
                e, f = ef // 4, ef % 4
                for h in range(2):
                    for k in range(2):
                        mm = pe.matmul(bank[2 * (ef % 2) + h][:, 0:CN // 2], lhsT=w1[:, e, k, f * P:(f + 1) * P],
                                       rhs=tT_all.rearrange("p c n -> p (c n)")[:, bass.ds(c * 2 * CN + k * CN + h * CN // 2, CN // 2)],
                                       start=(k == 0), stop=(k == 1))
                mm.then_inc(s["f_hidden"], 1)

            def products(c, ef):
                pe.wait_ge(s["f_gelu"], c * 8 + ef + 1)
                for b in range(CB):
                    mm = pe.matmul(bank[4 + b // 2][:, (b % 2) * D:(b % 2 + 1) * D], lhsT=hT[:, ef % 2, b * P:(b + 1) * P],
                                   rhs=w2[:, ef // 4, ef % 4, :], start=(ef == 0 and b % 2 == 0), stop=(ef == 7), skip_group_check=True)
                mm.then_inc(s["f_rows"], 1)
                return mm

            def chunk(c, first=False):
                hidden(c, 0)
                if not first:
                    pe.wait_ge(s["f_norm_stats"], c)
                for ef in range(8):
                    if ef < 7:
                        hidden(c, ef + 1)
                    products(c, ef)
                pe.wait_ge(s["f_rows"], NC + c * 8 + 8)
                pe.transpose(bank[0][0:P, 0:P], m.ident[:, :], m.ident[:, :]).then_inc(s["f_products"], 1)

            chunk(0, first=True)
            with nc.tensor.Fori(1, NC) as c:
                chunk(c)


def build_program(nc, w, out):
    t = {
        "hi": nc.dram_tensor("source_hi", [E], F32, kind="Internal").ap(),
        "sorted": nc.dram_tensor("sorted_edges", [ROWS, RW], F32, kind="Internal").ap(),
        "x2": nc.dram_tensor("x_after_layer0", [NB * P, D], F32, kind="Internal").ap(),
        "kv": nc.dram_tensor("keys_values", [NB * P, 2 * D], F32, kind="Internal").ap(),
    }
    with ExitStack() as ctx:
        m = allocate(nc, ctx)
        histogram_and_sort(nc, m, t, w)
        edge_sums(nc, m, t)
        node_stage(nc, m, t, w)
        attention(nc, m, t)
        output_stage(nc, m, t, w, out)


INS = ["x", "src", "dst", "edge_attr_128", "node_vec1", "node_vec1_n2", "L0_gnn_z_in", "L0_gnn_z_out", "L0_gnn_W_cent",
       "L0_gnn_b_cent", "L0_gnn_W_vor", "L0_gnn_b_vor", "L0_gnn_W_sum", "L0_gnn_b_sum", "L0_ffn_router_w",
       "L0_ffn_w1", "L0_ffn_b1", "L0_ffn_w2", "L0_ffn_b2", "L1_gnn_Wq", "L1_gnn_bq", "L1_gnn_Wk", "L1_gnn_bk",
       "L1_gnn_Wv", "L1_gnn_bv", "L1_gnn_Wo", "L1_gnn_bo", "L1_ffn_Wr", "L1_ffn_br", "L1_ffn_W1", "L1_ffn_b1",
       "L1_ffn_W2", "L1_ffn_b2", "L1_ffn_gamma", "L1_ffn_beta"]


def kernel(**inputs):
    import numpy as _np
    import concourse.bacc as _bacc
    from concourse.bass_utils import run_bass_kernel_spmd as _run

    nc = _bacc.Bacc("TRN2", target_bir_lowering=False, num_devices=1)
    arrays, w = {}, {}
    for name in INS:
        a = _np.ascontiguousarray(inputs[name])
        arrays[f"in_{name}"] = a
        w[name] = nc.dram_tensor(f"in_{name}", a.shape, mybir.dt.from_np(a.dtype), kind="ExternalInput").ap()
    out = nc.dram_tensor("out_0", [N, D], F32, kind="ExternalOutput").ap()
    build_program(nc, w, out)
    r = _run(nc, [arrays], core_ids=[0])
    return r.results[0]["out_0"]
```
